# Optimizing a Trainium2 kernel written in Bass

```python
import numpy as np
import jax
import jax.numpy as jnp

def _softmax(x, axis=-1):
    return jax.nn.softmax(x, axis=axis)

def _gelu(x):
    return jax.nn.gelu(x, approximate=True)

def _silu(x):
    return jax.nn.silu(x)

def _sigmoid(x):
    return jax.nn.sigmoid(x)

def _layernorm(x, axis=-1, eps=1e-05):
    m = jnp.mean(x, axis=axis, keepdims=True)
    v = jnp.var(x, axis=axis, keepdims=True)
    return (x - m) / jnp.sqrt(v + eps)

def _scatter_add(tgt, idx, src, axis=0):
    return tgt.at[idx].add(src)

def _segment_sum(src, seg, n):
    return jax.ops.segment_sum(src, seg, n)
kernel_name = 'mk_xattn_ffn_d2_seqx_r8_326f0f'

def setup_inputs(seed: int=0):
    np.random.seed(seed)
    _w = jnp.asarray

    def _rec_inputs():
        import jax
        import jax.numpy as jnp
        _rk = jax.random.key(seed)
        x = 0.0002417 + 0.9998 * jax.random.normal(jax.random.fold_in(_rk, 1), (4, 512, 128), jnp.float32)
        _lenS = 512 - jax.random.randint(jax.random.fold_in(_rk, 7), (4,), 0, max(1, 512 // 4) + 1, jnp.int32)
        _lenS2 = 77 - jax.random.randint(jax.random.fold_in(_rk, 8), (4,), 0, max(1, 77 // 4) + 1, jnp.int32)
        _ctx_1024P = jax.random.normal(jax.random.fold_in(_rk, 11), (4, 16, 128), jnp.float32)
        _ctx_1024c = jax.random.dirichlet(jax.random.fold_in(_rk, 511), 0.3 * jnp.ones((16,), jnp.float32), (4, 77))
        _ctx_1024t = jnp.einsum('bsk,bkd->bsd', _ctx_1024c, _ctx_1024P)
        _ctx_1024t = _ctx_1024t * jax.lax.rsqrt(jnp.mean(jnp.square(_ctx_1024t)) + 1e-12) * 0.953939
        ctx_1024 = 7.22013e-05 + 1.00017 * (_ctx_1024t + 0.3 * jax.random.normal(jax.random.fold_in(_rk, 611), (4, 77, 128), jnp.float32))
        _validS = jnp.arange(512)[None, :] < _lenS[:, None]
        _validS2 = jnp.arange(77)[None, :] < _lenS2[:, None]
        _causal = jnp.tril(jnp.ones((512, 512), dtype=bool))
        mask_1xSxS2_bk0 = jnp.logical_not(jnp.broadcast_to(_validS2[0:1, None, :], (1, 512, 77)))
        mask_BxS2_if1 = jnp.where(jnp.ones((4, 77), dtype=bool), 1, 0).astype(jnp.int32)
        return (x, ctx_1024, mask_1xSxS2_bk0, mask_BxS2_if1)
    x, ctx_1024, mask_1xSxS2_bk0, mask_BxS2_if1 = _rec_inputs()

    def _L0_xattn_setup():
        import jax, jax.numpy as jnp
        import numpy as np
        B, S, D = (4, 256, 128)
        key = jax.random.key(seed)
        kv, kk, kq, kw = jax.random.split(key, 4)
        scale = 1.0 / np.sqrt(D)
        v = jax.random.normal(kv, (B, S, D), dtype=jnp.float32)
        k = jax.random.normal(kk, (B, S, D), dtype=jnp.float32)
        q = jax.random.normal(kq, (B, S, D), dtype=jnp.float32)
        wi = jax.random.normal(kw, (D, D), dtype=jnp.float32) * scale
        mask = jnp.tril(jnp.ones((S, S), dtype=bool))[None, :, :]
        return {'v': v, 'k': k, 'q': q, 'wi': wi, 'mask': mask}
    _L0_xattn_all = _L0_xattn_setup()
    _L0_xattn_in = {k: v for k, v in _L0_xattn_all.items() if k in ('wi',)}
    del _L0_xattn_all

    def _L0_ffn_setup():
        import jax, jax.numpy as jnp
        import numpy as np
        EPS = 1e-06
        TOP_K = 2

        def rms_norm(x, scale, eps=EPS):
            xf = x.astype(jnp.float32)
            mean_sq = jnp.mean(xf * xf, axis=-1, keepdims=True)
            return (xf * (scale.astype(jnp.float32) * jax.lax.rsqrt(mean_sq + eps))).astype(x.dtype)
        key = jax.random.key(seed)
        k0, k1, k2, k3 = jax.random.split(key, 4)
        B, S, D, H, E = (2, 256, 128, 352, 8)
        x = jax.random.normal(k0, (B, S, D), dtype=jnp.float32)
        norm_scale = jnp.ones((D,), dtype=jnp.float32)
        w_router = jax.random.normal(k1, (E, D), dtype=jnp.float32) * 0.02
        w_up = jax.random.normal(k2, (E, 2 * H, D), dtype=jnp.float32) * 0.02
        w_down = jax.random.normal(k3, (E, D, H), dtype=jnp.float32) * 0.02
        return {'x': x, 'norm_scale': norm_scale, 'w_router': w_router, 'w_up': w_up, 'w_down': w_down}
    _L0_ffn_all = _L0_ffn_setup()
    _L0_ffn_in = {k: v for k, v in _L0_ffn_all.items() if k in ('norm_scale', 'w_router', 'w_up', 'w_down')}
    del _L0_ffn_all

    def _L1_xattn_setup():
        import jax, jax.numpy as jnp
        import numpy as np
        NEG = -10000.0
        key = jax.random.key(seed)
        k1, k2, k3 = jax.random.split(key, 3)
        B, L, D, H = (16, 256, 128, 128)
        x1 = jax.random.normal(k1, (B, L, D), dtype=jnp.float32)
        x2 = jax.random.normal(k2, (B, L, D), dtype=jnp.float32)
        x2_mask = jnp.ones((B, L), dtype=jnp.int64)
        W = jax.random.normal(k3, (H, D), dtype=jnp.float32) * (1.0 / np.sqrt(D))
        diagonal = jnp.ones((H,), dtype=jnp.float32)
        return {'x1': x1, 'x2': x2, 'x2_mask': x2_mask, 'W': W, 'diagonal': diagonal}
    _L1_xattn_all = _L1_xattn_setup()
    _L1_xattn_in = {k: v for k, v in _L1_xattn_all.items() if k in ('W', 'diagonal')}
    del _L1_xattn_all

    def _L1_ffn_setup():
        import jax, jax.numpy as jnp
        import numpy as np
        DIM = 128

        def _reference_tuple_inner(x, W_r, W_k, W_v, mu_r, mu_k):
            B, T, C = x.shape
            x_prev = jnp.concatenate([jnp.zeros((B, 1, C), x.dtype), x[:, :-1, :]], axis=1)
            xr = mu_r * x + (1.0 - mu_r) * x_prev
            xk = mu_k * x + (1.0 - mu_k) * x_prev
            r = jax.nn.sigmoid(jnp.einsum('btc,dc->btd', xr, W_r))
            k = jnp.einsum('btc,dc->btd', xk, W_k)
            k_act = jnp.square(jax.nn.relu(k))
            out = r * jnp.einsum('btc,dc->btd', k_act, W_v)
            new_state = x[:, -1, :]
            return (out, new_state)
        key = jax.random.key(seed)
        ks = jax.random.split(key, 6)
        B, T, C = (8, 256, DIM)
        x = jax.random.normal(ks[0], (B, T, C), dtype=jnp.float32)
        s = 1.0 / np.sqrt(C)
        W_r = jax.random.uniform(ks[1], (C, C), jnp.float32, -s, s)
        W_k = jax.random.uniform(ks[2], (C, C), jnp.float32, -s, s)
        W_v = jax.random.uniform(ks[3], (C, C), jnp.float32, -s, s)
        mu_r = jax.random.uniform(ks[4], (C,), jnp.float32)
        mu_k = jax.random.uniform(ks[5], (C,), jnp.float32)
        return {'x': x, 'W_r': W_r, 'W_k': W_k, 'W_v': W_v, 'mu_r': mu_r, 'mu_k': mu_k}
    _L1_ffn_all = _L1_ffn_setup()
    _L1_ffn_in = {k: v for k, v in _L1_ffn_all.items() if k in ('W_r', 'W_k', 'W_v', 'mu_r', 'mu_k')}
    del _L1_ffn_all
    return {'x': x, 'ctx_1024': ctx_1024, 'mask_1xSxS2_bk0': mask_1xSxS2_bk0, 'mask_BxS2_if1': mask_BxS2_if1, 'L0_xattn_wi': _L0_xattn_in['wi'], 'L0_ffn_norm_scale': _L0_ffn_in['norm_scale'], 'L0_ffn_w_router': _L0_ffn_in['w_router'], 'L0_ffn_w_up': _L0_ffn_in['w_up'], 'L0_ffn_w_down': _L0_ffn_in['w_down'], 'L1_xattn_W': _L1_xattn_in['W'], 'L1_xattn_diagonal': _L1_xattn_in['diagonal'], 'L1_ffn_W_r': _L1_ffn_in['W_r'], 'L1_ffn_W_k': _L1_ffn_in['W_k'], 'L1_ffn_W_v': _L1_ffn_in['W_v'], 'L1_ffn_mu_r': _L1_ffn_in['mu_r'], 'L1_ffn_mu_k': _L1_ffn_in['mu_k']}

def reference(x, ctx_1024, mask_1xSxS2_bk0, mask_BxS2_if1, L0_xattn_wi, L0_ffn_norm_scale, L0_ffn_w_router, L0_ffn_w_up, L0_ffn_w_down, L1_xattn_W, L1_xattn_diagonal, L1_ffn_W_r, L1_ffn_W_k, L1_ffn_W_v, L1_ffn_mu_r, L1_ffn_mu_k):
    import jax
    import jax.numpy as jnp

    def _L0_xattn_ref(v, k, q, wi, mask):
        import jax, jax.numpy as jnp
        import numpy as np
        B, S, D = (4, 256, 128)
        q = q @ wi
        k = k @ wi
        v = v @ wi
        scores = jnp.einsum('bqd,bkd->bqk', q, k) / jnp.sqrt(jnp.asarray(q.shape[-1], q.dtype))
        scores = jnp.where(mask, scores, jnp.asarray(-10000000000.0, scores.dtype))
        attn = jax.nn.softmax(scores, axis=-1)
        return q + jnp.einsum('bqk,bkd->bqd', attn, v)

    def _L0_ffn_ref(x, norm_scale, w_router, w_up, w_down):
        import jax, jax.numpy as jnp
        import numpy as np
        EPS = 1e-06
        TOP_K = 2

        def rms_norm(x, scale, eps=EPS):
            xf = x.astype(jnp.float32)
            mean_sq = jnp.mean(xf * xf, axis=-1, keepdims=True)
            return (xf * (scale.astype(jnp.float32) * jax.lax.rsqrt(mean_sq + eps))).astype(x.dtype)
        skip = x
        xn = rms_norm(x, norm_scale)
        scores = jnp.einsum('bsd,ed->bse', xn, w_router)
        _, ids = jax.lax.top_k(scores, TOP_K)
        probs = jax.nn.softmax(scores, axis=-1)
        c = jnp.take_along_axis(probs, ids, axis=-1)
        h = jnp.einsum('bsd,ehd->bseh', xn, w_up)
        val, gate = jnp.split(h, 2, axis=-1)
        h = val * jax.nn.silu(gate)
        y = jnp.einsum('bseh,edh->bsed', h, w_down)
        yk = jnp.take_along_axis(y, ids[..., None], axis=2)
        out = jnp.sum(yk * c[..., None], axis=2)
        return out + skip

    def _L1_xattn_ref(x1, x2, x2_mask, W, diagonal):
        import jax, jax.numpy as jnp
        import numpy as np
        NEG = -10000.0
        x1_rep = jax.nn.relu(jnp.einsum('bld,hd->blh', x1, W))
        x2_rep = jax.nn.relu(jnp.einsum('bld,hd->blh', x2, W))
        scores = jnp.einsum('bih,bjh->bij', x1_rep * diagonal, x2_rep)
        m = (1.0 - x2_mask.astype(scores.dtype)) * NEG
        alpha = jax.nn.softmax(scores + m[:, None, :], axis=-1)
        return jnp.einsum('bij,bjd->bid', alpha, x2)

    def _L1_ffn_ref(x, W_r, W_k, W_v, mu_r, mu_k):
        import jax, jax.numpy as jnp
        import numpy as np
        DIM = 128

        def _reference_tuple_inner(x, W_r, W_k, W_v, mu_r, mu_k):
            B, T, C = x.shape
            x_prev = jnp.concatenate([jnp.zeros((B, 1, C), x.dtype), x[:, :-1, :]], axis=1)
            xr = mu_r * x + (1.0 - mu_r) * x_prev
            xk = mu_k * x + (1.0 - mu_k) * x_prev
            r = jax.nn.sigmoid(jnp.einsum('btc,dc->btd', xr, W_r))
            k = jnp.einsum('btc,dc->btd', xk, W_k)
            k_act = jnp.square(jax.nn.relu(k))
            out = r * jnp.einsum('btc,dc->btd', k_act, W_v)
            new_state = x[:, -1, :]
            return (out, new_state)
        return _reference_tuple_inner(x, W_r, W_k, W_v, mu_r, mu_k)[0]
    x = x + _L0_xattn_ref(ctx_1024, ctx_1024, _layernorm(x, axis=-1), L0_xattn_wi, mask_1xSxS2_bk0)
    x = x + _L0_ffn_ref(_layernorm(x, axis=-1), L0_ffn_norm_scale, L0_ffn_w_router, L0_ffn_w_up, L0_ffn_w_down)
    x = x + _L1_xattn_ref(_layernorm(x, axis=-1), ctx_1024, mask_BxS2_if1, L1_xattn_W, L1_xattn_diagonal)
    x = x + _L1_ffn_ref(_layernorm(x, axis=-1), L1_ffn_W_r, L1_ffn_W_k, L1_ffn_W_v, L1_ffn_mu_r, L1_ffn_mu_k)
    return x

_drawn_inputs = setup_inputs


def setup_inputs(seed=0):
    import zlib

    import numpy as np

    out = dict(_drawn_inputs(seed))
    spreads = {'L0_ffn_norm_scale': (1.0, 0.6), 'L1_xattn_diagonal': (1.0, 0.2)}
    factors = {'L0_ffn_w_router': 8.0,
     'L0_ffn_w_up': 8.0,
     'L0_ffn_w_down': 8.0,
     'L1_ffn_W_r': 7.044,
     'L1_ffn_mu_r': 8.0,
     'L1_ffn_mu_k': 3.616}
    for name, (base, spread) in spreads.items():
        noise = np.random.default_rng([zlib.crc32(name.encode()), seed]).standard_normal(out[name].shape)
        drawn = base * np.exp(spread * noise) if base else spread * noise
        out[name] = jnp.asarray(drawn.astype(out[name].dtype))
    for name, factor in factors.items():
        out[name] = (out[name] * factor).astype(out[name].dtype)
    return out
```

```python
from contextlib import ExitStack

import numpy as np
import concourse.bass as bass
from concourse import mybir

F32 = mybir.dt.float32
F16 = mybir.dt.float16
I32 = mybir.dt.int32
U8 = mybir.dt.uint8
ALU = mybir.AluOpType
ACT = mybir.ActivationFunctionType
AX = mybir.AxisListType

P = 128
B, S, D = 4, 512, 128
J = 77
E, H = 8, 352
K = 2
T = B * S
TILES = T // P
G = S // P
PAIRS = K * T
BLOCKS = (PAIRS + E * (P - 1)) // P
HC = (H + P - 1) // P
HP = HC * P
H_LAST = H - (HC - 1) * P
SLOTS = BLOCKS * P
CREDIT = 16
RING = 4
LAG = 2
LN_EPS, RMS_EPS = 1e-5, 1e-6
MASKED = -1e10
FREE = 3.0e38

C_IDENT = 0
C_IOTA = C_IDENT + P
C_FIRST = C_IOTA + P
C_LOWER = C_FIRST + TILES * E
C_BLOCK = C_LOWER + E * E
C_SPARE = C_BLOCK + BLOCKS
C_PAIR = C_SPARE + BLOCKS
C_STEP = C_PAIR + K * TILES
C_ALL = C_STEP + T // P
M_BEFORE = 0
M_ONES = M_BEFORE + P
M_EARLIER = M_ONES + P
M_SAME = M_EARLIER + TILES * E
M_ALL = M_SAME + E


def build(nc, x, ctx, ctx_t, attn_mask, row_mask, wi, wi_t, norm_scale, router_t, up_t, down_t,
          w1_t, diagonal, wr_t, wk_t, wv_t, mu_r, mu_k, consts, zero_ones, out):
    with ExitStack() as stack:
        def sb(name, shape, dt=F32):
            return stack.enter_context(nc.sbuf_tensor(name, shape, dt))

        def sem(name):
            return stack.enter_context(nc.semaphore(name))

        xn_dram = nc.dram_tensor("xn_rows", [T, D], F32).ap()
        y_dram = nc.dram_tensor("y_rows", [PAIRS + SLOTS, D], F32).ap()

        banks = [stack.enter_context(nc.psum_tensor(f"bank{n}", [P, 512], F32)) for n in range(8)]

        cst = sb("cst", [P, C_ALL])
        m01 = sb("m01", [P, M_ALL], F16)
        ident = cst[:, C_IDENT:C_IDENT + P]
        iota = cst[:, C_IOTA:C_IOTA + P]
        first_w = cst[:, C_FIRST:C_FIRST + TILES * E].rearrange("p (t e) -> p t e", e=E)
        lower = cst[:, C_LOWER:C_LOWER + E * E].rearrange("p (e f) -> p e f", f=E)
        block_no = cst[:, C_BLOCK:C_BLOCK + BLOCKS]
        spare_row = cst[:, C_SPARE:C_SPARE + BLOCKS]
        pair_no = cst[:, C_PAIR:C_PAIR + K * TILES]
        step_no = cst[:, C_STEP:C_STEP + T // P]
        ctx_sb = sb("ctx_sb", [J, B, D])
        ctx_t_sb = sb("ctx_t_sb", [P, B * J])
        mask_sb = sb("mask_sb", [P, G, J], U8)
        row_mask_sb = sb("row_mask_sb", [1, B * J], I32)
        wi_sb = sb("wi_sb", [P, D])
        wi_t_sb = sb("wi_t_sb", [P, D])
        scale_sb = sb("scale_sb", [P, 1])
        router_sb = sb("router_sb", [P, E])
        up_sb = sb("up_sb", [P, E, 2 * H])
        down_sb = sb("down_sb", [P, HC, E, D])
        w1_sb = sb("w1_sb", [P, D])
        diag_sb = sb("diag_sb", [P, 1])
        wr_sb = sb("wr_sb", [P, D])
        wk_sb = sb("wk_sb", [P, D])
        wv_sb = sb("wv_sb", [P, D])
        mu_r_sb = sb("mu_r_sb", [P, 1])
        mu_k_sb = sb("mu_k_sb", [P, 1])
        power = sb("power", [P, G])

        kt0 = sb("kt0", [P, B * J])
        qs_rhs = sb("qs_rhs", [P, B, D + J])
        v0 = sb("v0", [J, B, D])
        cap = sb("cap", [P, G, J])
        router_s = sb("router_s", [P, E])
        k1 = sb("k1", [P, B, J])
        add1 = sb("add1", [1, B, G, J])
        add1_b = sb("add1_b", [1, B * J])
        ones_row = sb("ones_row", [1, P])

        def two(name, shape, dt=F32):
            return [sb(f"{name}{q}", shape, dt) for q in range(2)]

        xg = two("xg", [P, G, D])
        stats = two("stats", [P, G, 6])
        both = two("both", [P, G, 3])
        apart = two("apart", [P, G])
        mean = two("mean", [P, G])
        ve = two("ve", [P, G])
        rstd = two("rstd", [P, G])
        xh = two("xh", [P, G, D])
        xt = two("xt", [P, S + 1])
        sm = two("sm", [P, G, J])
        nmax = two("nmax", [P, G])
        pr = two("pr", [P, G, J])
        rsum = two("rsum", [P, G])
        rinv = two("rinv", [P, G])
        pt = two("pt", [J, S])
        x1 = two("x1", [P, G, D])
        mean2 = two("mean2", [P, G])
        var2 = two("var2", [P, G])
        rstd2 = two("rstd2", [P, G])
        ms = two("ms", [P, G])
        rms = two("rms", [P, G])
        yl = two("yl", [P, G, D])
        xn = two("xn", [P, G, D])
        skip = sb("skip", [P, TILES, D])

        def route(name, shape=(P, TILES, E), dt=F32):
            return sb(name, list(shape), dt)

        sc, eq, sc2, big1, big2, hot1, hot2, dist = (route(n) for n in (
            "sc", "eq", "sc2", "big1", "big2", "hot1", "hot2", "dist"))
        top1, top2, pick1, pick2, den, c_rec = (route(n, (P, TILES)) for n in (
            "top1", "top2", "pick1", "pick2", "den", "c_rec"))
        weight = route("weight", (P, TILES, K))
        hot = route("hot", dt=F16)
        counts = sb("counts", [P, P], F16)
        n_gt = sb("n_gt", [P, E, T // P])
        n_blocks = sb("n_blocks", [P, E])
        tri = sb("tri", [P, E, E])
        start_blk = sb("start_blk", [P, E])
        end_blk = sb("end_blk", [P, E])
        start_pos = sb("start_pos", [P, E])
        pos_e = route("pos_e")
        pos_m = sb("pos_m", [P, K, TILES, E])
        pos = sb("pos", [P, K * TILES])
        pos_i = sb("pos_i", [P, K * TILES], I32)
        blk_i = sb("blk_i", [P, K * TILES], I32)
        row_i = sb("row_i", [P, K * TILES], I32)
        blk_f = sb("blk_f", [P, K * TILES])
        row_f = sb("row_f", [P, K * TILES])
        in_block = sb("in_block", [P, K * TILES, BLOCKS])
        in_row = sb("in_row", [P, K * TILES, P])
        past = sb("past", [1, BLOCKS, E])
        expert_f = sb("expert_f", [1, BLOCKS])
        expert = sb("expert", [1, BLOCKS], I32)
        pair_f = sb("pair_f", [P, BLOCKS])
        second = sb("second", [P, BLOCKS])
        empty = sb("empty", [P, BLOCKS])
        spare = sb("spare", [P, BLOCKS])
        src_row = sb("src_row", [P, BLOCKS], I32)
        dst_row = sb("dst_row", [P, BLOCKS], I32)

        rows = [sb(f"rows{m}", [P, D]) for m in range(RING)]
        rows_t = two("rows_t", [P, P])
        th = two("th", [P, H])
        gs = two("gs", [P, H])
        hid = two("hid", [P, HP])
        hid_t = two("hid_t", [P, HP])
        ys = [sb(f"ys{m}", [P, D]) for m in range(RING)]

        yb = two("yb", [P, K, G, D])
        x2 = two("x2", [P, G, D])
        rt = two("rt", [P, S])
        x3 = two("x3", [P, G, D])
        dz = two("dz", [P, S])
        xr = two("xr", [P, S])
        xk = two("xk", [P, S])
        rk = two("rk", [P, S])
        ka = two("ka", [P, S])
        tg = two("tg", [P, G * D])
        wv = two("wv", [P, G * D])
        res = two("res", [P, G * D])

        NAMES = """consts_in weights0_in mask_in experts_in weights1_in zeroed
            kt0_mm kt0_sb qs_mm v0_mm k1_mm v0_sb setup_dve setup_act
            st_done ve_done rstd_done xh_done xt_mm xt_done qs_done sm_done max_done exp_done rinv_done
            pr_done pt_mm pt_done pv_done x1_done st2_done ve2_done rstd2_done ms_done rms_done
            yl_done xn_done xn_mm xnt_done rt_done skip_done
            r_step hot_done prefix_mm counts_done totals_mm dist_done ex_done pos_ready inrow_done
            inv_mm src_done dst_done expert_done
            b_xt_mm b_xt b_up b_th b_gs b_hid b_ht_mm b_ht b_dn b_y ys_free
            c_prod c_sum c_x2 c_st c_ve c_rstd c_xh c_xt_mm c_xt c_rt_mm c_rt c_sc c_max c_exp c_rinv c_pt_mm
            c_pt c_pv c_x3 c_st4 c_ve4 c_rstd4 c_z c_zt_mm c_zt c_dz c_xr c_xk c_k c_r c_rk c_ka
            c_tg c_kv c_wv c_res""".split()
        s = {n: sem(n) for n in NAMES}
        x_in = [sem(f"x_in{q}") for q in range(2)]
        xn_out = [sem(f"xn_out{q}") for q in range(2)]
        rows_in = [sem(f"rows_in{m}") for m in range(RING)]
        ys_out = [sem(f"ys_out{m}") for m in range(RING)]
        yb_in = [sem(f"yb_in{q}") for q in range(2)]
        res_out = [sem(f"res_out{q}") for q in range(2)]

        def scores0(q):
            return [banks[2 * q + h][:, 0:2 * (D + J)].rearrange("p (t c) -> p t c", t=2)
                    for h in range(2)]

        def tiles_in(dram, n):
            return dram[bass.ds(n * S, S), :].rearrange("(t p) d -> p t d", p=P)

        trans = [banks[4], banks[5]]
        route_bank = banks[6]
        block = stack.enter_context(nc.Block())

        @block.sync
        def _(sp):
            for free in (*xn_out, *res_out):
                sp.sem_inc(free, CREDIT)
            for q in range(2):
                sp.dma_start(xg[q][:], tiles_in(x, q)).then_inc(x_in[q], 16)
                if q == 0:
                    sp.dma_start(wi_sb[:], wi).then_inc(s["weights0_in"], 16)
                    sp.dma_start(ctx_t_sb[:], ctx_t).then_inc(s["weights0_in"], 16)
                    sp.dma_start(wi_t_sb[:], wi_t).then_inc(s["weights0_in"], 16)
                    sp.dma_start(cst[:], consts).then_inc(s["consts_in"], 16)
            sp.dma_start(router_sb[:], router_t).then_inc(s["weights0_in"], 16)
            sp.dma_start(scale_sb[:], norm_scale).then_inc(s["weights0_in"], 16)
            for n in range(2, B):
                sp.wait_ge(s["x1_done"], n - 1)
                sp.wait_ge(x_in[n % 2], 16)
                sp.dma_start(xg[n % 2][:], tiles_in(x, n)).then_inc(x_in[n % 2], 16)
                sp.wait_ge(s["xn_done"], n - 1)
                sp.dma_start(tiles_in(xn_dram, n - 2), xn[n % 2][:]).then_inc(xn_out[n % 2], 16)
            for n in range(2, B):
                sp.wait_ge(s["xn_done"], n + 1)
                sp.dma_start(tiles_in(xn_dram, n), xn[n % 2][:]).then_inc(xn_out[n % 2], 16)
            for m in range(RING):
                sp.wait_ge(ys_out[m], 16 * ((BLOCKS - m + RING - 1) // RING))
            for n in range(B):
                if n >= 2:
                    sp.wait_ge(s["c_sum"], n - 1)
                for k in range(K):
                    sp.dma_start(yb[n % 2][:, k], tiles_in(y_dram[k * T:(k + 1) * T, :], n)
                                 ).then_inc(yb_in[n % 2], 16)
            for n in range(B):
                sp.wait_ge(s["c_res"], n + 1)
                sp.dma_start(tiles_in(out, n), res[n % 2][:].rearrange("p (t d) -> p t d", d=D)
                             ).then_inc(res_out[n % 2], 16)
            for q in range(2):
                sp.wait_ge(res_out[q], CREDIT + 16 * (B // 2))
                sp.wait_ge(xn_out[q], CREDIT + 16 * (B // 2))

        @block.gpsimd
        def _(pool):
            pool.dma_start(mask_sb[:], attn_mask).then_inc(s["mask_in"], 16)
            pool.dma_start(row_mask_sb[:], row_mask).then_inc(s["mask_in"], 16)
            nc.gpsimd.memset(power[:], -0.5)
            for m in range(2):
                nc.gpsimd.memset(hid[m][:, H:HP], 0.0)
            nc.gpsimd.memset(ones_row[:], 1.0).then_inc(s["zeroed"], 1)
            pool.wait_ge(s["zeroed"], 1)
            pool.sem_inc(s["ys_free"], RING)

            def rstd0(n, q):
                pool.wait_ge(s["ve_done"], n + 1)
                nc.gpsimd.tensor_tensor(rstd[q][:], ve[q][:], power[:], ALU.pow).then_inc(s["rstd_done"], 1)

            def rstd_y(n, q):
                pool.wait_ge(s["ve2_done"], n + 1)
                nc.gpsimd.tensor_tensor(rstd2[q][:], ve[q][:], power[:], ALU.pow).then_inc(s["rstd2_done"], 1)

            def rms_y(n, q):
                pool.wait_ge(s["ms_done"], n + 1)
                nc.gpsimd.tensor_tensor(rms[q][:], ms[q][:], power[:], ALU.pow).then_inc(s["rms_done"], 1)

            def skip0(n, q):
                pool.wait_ge(s["yl_done"], n + 1)
                nc.gpsimd.tensor_tensor(skip[:, bass.ds(n * G, G), :], x1[q][:], yl[q][:], ALU.add
                                        ).then_inc(s["skip_done"], 1)

            with pool.Fori(0, B - 1, 2) as i:
                for q in range(2):
                    rstd0(i + q, q)
                for q in range(2):
                    rstd_y(i + q, q)
                for q in range(2):
                    rms_y(i + q, q)
                for q in range(2):
                    skip0(i + q, q)

            def gather(b):
                if b >= RING:
                    pool.wait_ge(s["b_xt_mm"], b - RING + 1)
                pool.indirect_dma_start(
                    out=rows[b % RING][:], out_offset=None, in_=xn_dram,
                    in_offset=bass.IndirectOffsetOnAxis(ap=src_row[:, b:b + 1], axis=0),
                ).then_inc(rows_in[b % RING], 16)

            def scatter(b):
                if b >= LAG:
                    pool.wait_ge(ys_out[(b - LAG) % RING], 16 * ((b - LAG) // RING + 1))
                    pool.sem_inc(s["ys_free"], 1)
                pool.wait_ge(s["b_y"], 1 + b + 1)
                pool.indirect_dma_start(
                    out=y_dram, out_offset=bass.IndirectOffsetOnAxis(ap=dst_row[:, b:b + 1], axis=0),
                    in_=ys[b % RING][:], in_offset=None,
                ).then_inc(ys_out[b % RING], 16)

            pool.wait_ge(s["src_done"], 1)
            for q in range(2):
                pool.wait_ge(xn_out[q], CREDIT + 16 * (B // 2))
            for b in range(RING):
                gather(b)
            pool.wait_ge(s["dst_done"], 1)
            for b in range(RING, BLOCKS):
                gather(b)
                if b - RING - 3 >= 0:
                    scatter(b - RING - 3)
            for b in range(BLOCKS - RING - 3, BLOCKS):
                scatter(b)

            def combine(n, q):
                pool.wait_ge(yb_in[q], i * 16 + 32)
                for k in range(K):
                    ins = nc.gpsimd.tensor_tensor(
                        yb[q][:, k], yb[q][:, k],
                        weight[:, bass.ds(n * G, G), k:k + 1].to_broadcast([P, G, D]), ALU.mult)
                ins.then_inc(s["c_prod"], 1)
                pool.wait_ge(s["c_prod"], n + 1)
                nc.gpsimd.tensor_tensor(x2[q][:], yb[q][:, 0], yb[q][:, 1], ALU.add).then_inc(s["c_sum"], 1)
                pool.wait_ge(s["c_sum"], n + 1)
                nc.gpsimd.tensor_tensor(x2[q][:], x2[q][:], skip[:, bass.ds(n * G, G), :], ALU.add
                                        ).then_inc(s["c_x2"], 1)

            def rstd3(n, q):
                pool.wait_ge(s["c_ve"], n + 1)
                nc.gpsimd.tensor_tensor(rstd[q][:], ve[q][:], power[:], ALU.pow).then_inc(s["c_rstd"], 1)

            def rstd4(n, q):
                pool.wait_ge(s["c_ve4"], n + 1)
                nc.gpsimd.tensor_tensor(rstd2[q][:], ve[q][:], power[:], ALU.pow).then_inc(s["c_rstd4"], 1)

            def shift(n, q):
                pool.wait_ge(s["c_zt"], n + 1)
                nc.gpsimd.tensor_tensor(dz[q][:], xt[q][:, 1:S + 1], xt[q][:, 0:S], ALU.subtract
                                        ).then_inc(s["c_dz"], 1)

            with pool.Fori(0, B - 1, 2) as i:
                for stage in (combine, rstd3, rstd4, shift):
                    for q in range(2):
                        stage(i + q, q)

        @block.tensor
        def _(pe):
            mm = nc.tensor.matmul
            pe.wait_ge(s["weights0_in"], 16 * 5)
            mm(banks[0][:, 0:B * J], wi_sb[:], ctx_t_sb[:], start=True, stop=True).then_inc(s["kt0_mm"], 1)
            for b in range(B):
                last = mm(banks[1][0:J, b * D:(b + 1) * D], ctx_t_sb[:, b * J:(b + 1) * J], wi_sb[:],
                          start=True, stop=True)
            last.then_inc(s["v0_mm"], 1)
            pe.wait_ge(s["weights1_in"], 16 * 8)
            mm(banks[3][:, 0:B * J], w1_sb[:], ctx_t_sb[:], start=True, stop=True).then_inc(s["k1_mm"], 1)
            pe.wait_ge(s["kt0_sb"], 1)
            mm(banks[2][:, 0:B * J], wi_t_sb[:], kt0[:], start=True, stop=True).then_inc(s["qs_mm"], 1)
            pe.wait_ge(s["setup_dve"], 1)
            pe.wait_ge(s["setup_act"], 1)
            pe.wait_ge(s["consts_in"], 32)

            def transpose_group(n, q, src, ready, signal, rows_out=P):
                pe.wait_ge(s[ready], n + 1)
                for t in range(G):
                    last = nc.tensor.transpose(trans[q][0:rows_out, t * P:(t + 1) * P], src[q][:, t, :], ident)
                last.then_inc(s[signal], 1)

            def t_xh(n, q):
                transpose_group(n, q, xh, "xh_done", "xt_mm")

            def qs(n, q):
                pe.wait_ge(s["xt_done"], n + 1)
                rhs = qs_rhs[:, bass.ds(n, 1), :].rearrange("p o c -> p (o c)")
                for t in range(G):
                    last = mm(scores0(q)[t // 2][:, t % 2, :], xt[q][:, 1 + t * P:1 + (t + 1) * P], rhs,
                              start=(t % 2 == 0), stop=(t % 2 == 1), skip_group_check=True)
                last.then_inc(s["qs_done"], 1)

            def t_pr(n, q):
                transpose_group(n, q, pr, "pr_done", "pt_mm", J)

            def pv(n, q):
                pe.wait_ge(s["pt_done"], n + 1)
                rhs = v0[:, bass.ds(n, 1), :].rearrange("p o c -> p (o c)")
                for t in range(G):
                    last = mm(scores0(q)[t // 2][:, t % 2, 0:D], pt[q][:, t * P:(t + 1) * P], rhs,
                              start=False, stop=True, skip_group_check=True)
                last.then_inc(s["pv_done"], 1)

            def t_xn(n, q):
                transpose_group(n, q, xn, "xn_done", "xn_mm")

            def router(n, q):
                pe.wait_ge(s["xnt_done"], n + 1)
                for t in range(G):
                    last = mm(route_bank[:, bass.ds(n * G * E + t * E, E)], xt[q][:, 1 + t * P:1 + (t + 1) * P],
                              router_s[:], start=True, stop=True)
                last.then_inc(s["rt_done"], 1)

            with pe.Fori(0, B - 1, 2) as i:
                for stage in (t_xh, qs, t_pr, pv, t_xn, router):
                    for q in range(2):
                        stage(i + q, q)

            prefix = banks[0][:, 0:TILES * E]
            pe.wait_ge(s["hot_done"], 1)
            hot2d = hot[:].rearrange("p t e -> p (t e)")
            mm(banks[1][:, 0:P], hot2d, m01[:, M_ONES:M_ONES + P], start=True, stop=True).then_inc(s["prefix_mm"], 1)
            mm(prefix, m01[:, M_BEFORE:M_BEFORE + P], hot2d, start=True, stop=False)
            pe.wait_ge(s["counts_done"], 1)
            mm(banks[2][:, 0:E], counts[:], m01[:, M_SAME:M_SAME + E], start=True, stop=True)
            mm(prefix, counts[:], m01[:, M_EARLIER:M_EARLIER + TILES * E], start=False, stop=True
               ).then_inc(s["totals_mm"], 1)
            for c in range(K * TILES):
                pe.wait_ge(s["inrow_done"], c + 1)
                last = mm(banks[3][:, 0:BLOCKS], in_row[:, c, :], in_block[:, c, :],
                          start=(c == 0), stop=(c == K * TILES - 1))
            last.then_inc(s["inv_mm"], 1)

            gate = [banks[0], banks[1]]
            val = [banks[2], banks[3]]
            rt_bank, ht_bank, y_bank = banks[4], [banks[5], banks[6]], banks[7]

            def t_rows(b, b_mod, landed):
                pe.wait_ge(rows_in[b_mod % RING], landed)
                nc.tensor.transpose(rt_bank[:, 0:P], rows[b_mod % RING][:], ident).then_inc(s["b_xt_mm"], 1)

            def expert_of(b):
                return pe.value_load(expert[0:1, bass.ds(b, 1)], min_val=0, max_val=E - 1)

            def up(b, par):
                e = expert_of(b)
                pe.wait_ge(s["b_xt"], b + 1)
                for dst, at in ((gate[par], H), (val[par], 0)):
                    last = mm(dst[:, 0:H], rows_t[par][:],
                              up_sb[:, bass.ds(e, 1), at:at + H].rearrange("p o c -> p (o c)"),
                              start=True, stop=True)
                last.then_inc(s["b_up"], 1)

            def t_hid(b, par):
                pe.wait_ge(s["b_hid"], b + 1)
                for c in range(HC):
                    last = nc.tensor.transpose(ht_bank[par][:, c * P:(c + 1) * P],
                                               hid[par][:, c * P:(c + 1) * P], ident)
                last.then_inc(s["b_ht_mm"], 1)

            def down(b, par):
                e = expert_of(b)
                pe.wait_ge(s["b_ht"], b + 1)
                pe.wait_ge(s["b_y"], 1 + b)
                for c in range(HC):
                    kk = P if c < HC - 1 else H_LAST
                    last = mm(y_bank[:, 0:D], hid_t[par][0:kk, c * P:(c + 1) * P],
                              down_sb[0:kk, c, bass.ds(e, 1), :].rearrange("p o c -> p (o c)"),
                              start=(c == 0), stop=(c == HC - 1))
                last.then_inc(s["b_dn"], 1)

            pe.wait_ge(s["expert_done"], 1)
            pe.wait_ge(s["dst_done"], 1)
            pe.wait_ge(s["experts_in"], 16 * (E + 2))
            t_rows(0, 0, 16)
            up(0, 0)
            t_rows(1, 1, 16)
            up(1, 1)
            t_hid(0, 0)
            t_rows(2, 2, 16)
            with pe.Fori(2, BLOCKS - RING, RING) as i:
                for j in range(RING):
                    b, m = i + j, (2 + j) % RING
                    up(b, m % 2)
                    down(b - 2, m % 2)
                    t_hid(b - 1, (m + 1) % 2)
                    t_rows(b + 1, m + 1, (i + (j + 1 - (m + 1) % RING)) * 4 + 16)
            b = BLOCKS - 1
            up(b, b % 2)
            down(b - 2, b % 2)
            t_hid(b - 1, (b - 1) % 2)
            down(b - 1, (b - 1) % 2)
            t_hid(b, b % 2)
            down(b, b % 2)

            proj, attn, mix = [banks[0], banks[1]], [banks[2], banks[3]], [banks[6], banks[7]]

            def c_t_xh(n, q):
                transpose_group(n, q, xh, "c_xh", "c_xt_mm")

            def c_rt(n, q):
                pe.wait_ge(s["c_xt"], n + 1)
                mm(proj[q][:], w1_sb[:], xt[q][:, 1:S + 1], start=True, stop=True).then_inc(s["c_rt_mm"], 1)

            def c_scores(n, q):
                pe.wait_ge(s["c_rt"], n + 1)
                mm(attn[q][:, 0:G * J], ones_row[:],
                   add1[:, bass.ds(n, 1), :, :].rearrange("p o t j -> p (o t j)"),
                   start=True, stop=False, skip_group_check=True)
                rhs = k1[:, bass.ds(n, 1), :].rearrange("p o j -> p (o j)")
                for t in range(G):
                    last = mm(attn[q][:, t * J:(t + 1) * J], rt[q][:, t * P:(t + 1) * P], rhs,
                              start=False, stop=(t == G - 1), skip_group_check=True)
                last.then_inc(s["c_sc"], 1)

            def c_t_pr(n, q):
                transpose_group(n, q, pr, "c_exp", "c_pt_mm", J)

            def c_pv(n, q):
                pe.wait_ge(s["c_pt"], n + 1)
                rhs = ctx_sb[:, bass.ds(n, 1), :].rearrange("p o c -> p (o c)")
                for t in range(G):
                    last = mm(mix[q][:, t * D:(t + 1) * D], pt[q][:, t * P:(t + 1) * P], rhs,
                              start=True, stop=True)
                last.then_inc(s["c_pv"], 1)

            def c_t_z(n, q):
                transpose_group(n, q, xh, "c_z", "c_zt_mm")

            def c_k(n, q):
                pe.wait_ge(s["c_xk"], n + 1)
                mm(proj[q][:], wk_sb[:], xk[q][:], start=True, stop=True).then_inc(s["c_k"], 1)

            def c_r(n, q):
                pe.wait_ge(s["c_xr"], n + 1)
                for t in range(G):
                    last = mm(attn[q][:, t * D:(t + 1) * D], xr[q][:, t * P:(t + 1) * P], wr_sb[:],
                              start=True, stop=True)
                last.then_inc(s["c_r"], 1)

            def c_kv(n, q):
                pe.wait_ge(s["c_ka"], n + 1)
                for t in range(G):
                    last = mm(mix[q][:, t * D:(t + 1) * D], ka[q][:, t * P:(t + 1) * P], wv_sb[:],
                              start=True, stop=True)
                last.then_inc(s["c_kv"], 1)

            with pe.Fori(0, B - 1, 2) as i:
                for stage in (c_t_xh, c_rt, c_scores, c_t_pr, c_pv, c_t_z, c_k, c_r, c_kv):
                    for q in range(2):
                        stage(i + q, q)

        @block.scalar
        def _(act):
            act.dma_start(m01[:], zero_ones).then_inc(s["consts_in"], 16)
            for dst, src in ((w1_sb, w1_t), (diag_sb, diagonal), (wr_sb, wr_t), (wk_sb, wk_t), (wv_sb, wv_t),
                             (mu_r_sb, mu_r), (mu_k_sb, mu_k), (ctx_sb, ctx)):
                act.dma_start(dst[:], src).then_inc(s["weights1_in"], 16)
            for e in range(E):
                act.dma_start(up_sb[:, e, :], up_t[:, e, :]).then_inc(s["experts_in"], 16)
            act.dma_start(down_sb[:, 0:HC - 1], down_t[0:(HC - 1) * P].rearrange("(c p) e d -> p c e d", p=P)
                          ).then_inc(s["experts_in"], 16)
            act.dma_start(down_sb[0:H_LAST, HC - 1], down_t[(HC - 1) * P:H]).then_inc(s["experts_in"], 16)

            act.wait_ge(s["kt0_mm"], 1)
            nc.scalar.activation(kt0[:], banks[0][:, 0:B * J], ACT.Copy).then_inc(s["kt0_sb"], 1)
            act.wait_ge(s["v0_mm"], 1)
            nc.scalar.activation(v0[:], banks[1][0:J, :].rearrange("p (b d) -> p b d", d=D), ACT.Copy)
            act.wait_ge(s["qs_mm"], 1)
            nc.scalar.activation(qs_rhs[:, :, D:D + J], banks[2][:, 0:B * J].rearrange("p (b j) -> p b j", j=J),
                                 ACT.Copy, scale=float(D) ** -0.5).then_inc(s["setup_act"], 1)

            def move_t(n, q, ready, signal):
                act.wait_ge(s[ready], n + 1)
                nc.scalar.activation(xt[q][:, 1:S + 1], trans[q][:], ACT.Copy).then_inc(s[signal], 1)

            def move_pt(n, q, ready, signal):
                act.wait_ge(s[ready], n + 1)
                nc.scalar.activation(pt[q][:], trans[q][0:J, :], ACT.Copy).then_inc(s[signal], 1)

            def exps(n, q, src, ready, signal):
                act.wait_ge(s[ready], n + 1)
                for t in range(G):
                    last = nc.scalar.activation(pr[q][:, t, :], src(t), ACT.Exp, bias=nmax[q][:, t:t + 1],
                                                accum_out=rsum[q][:, t:t + 1])
                last.then_inc(s[signal], 1)

            with act.Fori(0, B - 1, 2) as i:
                for q in range(2):
                    move_t(i + q, q, "xt_mm", "xt_done")
                for q in range(2):
                    exps(i + q, q, lambda t: sm[q][:, t, :], "max_done", "exp_done")
                for q in range(2):
                    move_pt(i + q, q, "pt_mm", "pt_done")
                for q in range(2):
                    move_t(i + q, q, "xn_mm", "xnt_done")

            act.wait_ge(s["dist_done"], 1)
            nc.scalar.activation(dist[:], dist[:], ACT.Exp)
            nc.scalar.activation(top2[:], top2[:], ACT.Exp).then_inc(s["ex_done"], 1)

            gate = [banks[0], banks[1]]
            rt_bank, ht_bank = banks[4], [banks[5], banks[6]]

            def move_rows(b, par):
                act.wait_ge(s["b_xt_mm"], b + 1)
                nc.scalar.activation(rows_t[par][:], rt_bank[:, 0:P], ACT.Copy, scale=scale_sb[:]
                                     ).then_inc(s["b_xt"], 1)

            def tanh_gate(b, par):
                act.wait_ge(s["b_up"], b + 1)
                nc.scalar.activation(th[par][:], gate[par][:, 0:H], ACT.Tanh, scale=0.5).then_inc(s["b_th"], 1)

            def move_hid(b, par):
                act.wait_ge(s["b_ht_mm"], b + 1)
                nc.scalar.activation(hid_t[par][:], ht_bank[par][:, 0:HP], ACT.Copy).then_inc(s["b_ht"], 1)

            move_rows(0, 0)
            tanh_gate(0, 0)
            move_rows(1, 1)
            tanh_gate(1, 1)
            move_hid(0, 0)
            move_rows(2, 0)
            with act.Fori(2, BLOCKS - RING, RING) as i:
                for j in range(RING):
                    b, par = i + j, j % 2
                    tanh_gate(b, par)
                    move_hid(b - 1, 1 - par)
                    move_rows(b + 1, 1 - par)
            b = BLOCKS - 1
            tanh_gate(b, b % 2)
            move_hid(b - 1, (b - 1) % 2)
            move_hid(b, b % 2)

            proj, attn = [banks[0], banks[1]], [banks[2], banks[3]]

            def relu(n, q, dst, ready, signal):
                act.wait_ge(s[ready], n + 1)
                nc.scalar.activation(dst[q][:], proj[q][:], ACT.Relu).then_inc(s[signal], 1)

            def mix_r(n, q):
                act.wait_ge(s["c_dz"], n + 1)

            with act.Fori(0, B - 1, 2) as i:
                for q in range(2):
                    move_t(i + q, q, "c_xt_mm", "c_xt")
                for q in range(2):
                    relu(i + q, q, rt, "c_rt_mm", "c_rt")
                for q in range(2):
                    exps(i + q, q, lambda t: attn[q][:, t * J:(t + 1) * J], "c_max", "c_exp")
                for q in range(2):
                    move_pt(i + q, q, "c_pt_mm", "c_pt")
                for q in range(2):
                    move_t(i + q, q, "c_zt_mm", "c_zt")
                for q in range(2):
                    relu(i + q, q, rk, "c_k", "c_rk")
                for q in range(2):
                    act.wait_ge(s["c_r"], i + q + 1)
                    nc.scalar.activation(tg[q][:], attn[q][:], ACT.Tanh, scale=0.5).then_inc(s["c_tg"], 1)

        @block.vector
        def _(dve):
            v = nc.vector
            dve.sem_inc(s["b_y"], 1)

            dve.wait_ge(s["mask_in"], 32)
            v.tensor_scalar(cap[:], mask_sb[:], FREE, MASKED, ALU.mult, ALU.add)
            v.tensor_scalar(add1_b[:], row_mask_sb[:], 1e4, -1e4, ALU.mult, ALU.add).then_inc(s["r_step"], 1)
            dve.wait_ge(s["r_step"], 1)
            v.tensor_copy(add1[:], add1_b[:].rearrange("p (b o j) -> p b o j", b=B, o=1)
                          .to_broadcast([1, B, G, J]))
            for q in range(2):
                v.memset(xt[q][:, 0:1], 0.0)
            dve.wait_ge(s["weights0_in"], 16 * 5)
            v.tensor_scalar(router_s[:], router_sb[:], scale_sb[:], None, ALU.mult)
            for b in range(B):
                v.tensor_copy(qs_rhs[:, b, 0:D], wi_sb[:])
            dve.wait_ge(s["weights1_in"], 16 * 8)
            dve.wait_ge(s["k1_mm"], 1)
            v.tensor_scalar(k1[:], banks[3][:, 0:B * J].rearrange("p (b j) -> p b j", j=J), 0.0, diag_sb[:],
                            ALU.max, ALU.mult).then_inc(s["setup_dve"], 1)

            def stats_of(n, q, src, mean_q, names, var_q=None):
                for t in range(G):
                    last = v.bn_stats(stats[q][:, t, :], src[:, t, :])
                last.then_inc(s[names[0]], 1)
                dve.wait_ge(s[names[0]], 3 * n + 1)
                v.tensor_tensor(both[q][:], stats[q][:, :, 0:3], stats[q][:, :, 3:6], ALU.add)
                v.tensor_tensor(apart[q][:], stats[q][:, :, 1], stats[q][:, :, 4], ALU.subtract
                                ).then_inc(s[names[0]], 1)
                dve.wait_ge(s[names[0]], 3 * n + 2)
                v.tensor_tensor(apart[q][:], apart[q][:], apart[q][:], ALU.mult)
                v.tensor_scalar(ve[q][:], both[q][:, :, 2], 1.0 / D, LN_EPS, ALU.mult, ALU.add)
                if var_q is not None:
                    v.tensor_scalar(var_q[:], both[q][:, :, 2], 1.0 / D, None, ALU.mult)
                v.tensor_scalar(mean_q[:], both[q][:, :, 1], 0.5, None, ALU.mult).then_inc(s[names[0]], 1)
                dve.wait_ge(s[names[0]], 3 * n + 3)
                if var_q is not None:
                    v.scalar_tensor_tensor(var_q[:], apart[q][:], 0.25, var_q[:], ALU.mult, ALU.add)
                v.scalar_tensor_tensor(ve[q][:], apart[q][:], 0.25, ve[q][:], ALU.mult, ALU.add
                                       ).then_inc(s[names[1]], 1)

            def norm(q, dst, src, mean_q, rs):
                for t in range(G):
                    last = v.tensor_scalar(dst[:, t, :], src[:, t, :], mean_q[:, t:t + 1], rs[:, t:t + 1],
                                           ALU.subtract, ALU.mult)
                return last

            def a_stats(n, q):
                dve.wait_ge(x_in[q], i * 8 + 16)
                stats_of(n, q, xg[q], mean[q], ("st_done", "ve_done"))

            def a_norm(n, q):
                dve.wait_ge(s["rstd_done"], n + 1)
                norm(q, xh[q], xg[q], mean[q], rstd[q]).then_inc(s["xh_done"], 1)

            def a_mask(n, q):
                dve.wait_ge(s["qs_done"], n + 1)
                for h in range(2):
                    last = v.tensor_tensor(sm[q][:, 2 * h:2 * h + 2, :], scores0(q)[h][:, :, D:D + J],
                                           cap[:, 2 * h:2 * h + 2, :], ALU.min)
                last.then_inc(s["sm_done"], 1)
                dve.wait_ge(s["sm_done"], n + 1)
                v.tensor_reduce(nmax[q][:], sm[q][:], axis=AX.X, op=ALU.max, negate=True
                                ).then_inc(s["max_done"], 1)

            def a_soft(n, q):
                dve.wait_ge(s["exp_done"], n + 1)
                v.reciprocal(rinv[q][:], rsum[q][:]).then_inc(s["rinv_done"], 1)
                dve.wait_ge(s["rinv_done"], n + 1)
                v.tensor_tensor(pr[q][:], pr[q][:],
                                rinv[q][:].rearrange("p (t o) -> p t o", o=1).to_broadcast([P, G, J]),
                                ALU.mult).then_inc(s["pr_done"], 1)

            def a_res(n, q):
                dve.wait_ge(s["pv_done"], n + 1)
                for h in range(2):
                    last = v.tensor_tensor(x1[q][:, 2 * h:2 * h + 2, :], scores0(q)[h][:, :, 0:D],
                                           xg[q][:, 2 * h:2 * h + 2, :], ALU.add)
                last.then_inc(s["x1_done"], 1)
                dve.wait_ge(s["x1_done"], n + 1)
                stats_of(n, q, x1[q], mean2[q], ("st2_done", "ve2_done"), var2[q])

            def a_y(n, q):
                dve.wait_ge(s["rstd2_done"], n + 1)
                v.tensor_tensor(ms[q][:], var2[q][:], rstd2[q][:], ALU.mult).then_inc(s["r_step"], 1)
                dve.wait_ge(s["r_step"], 2 * n + 2)
                v.tensor_tensor(ms[q][:], ms[q][:], rstd2[q][:], ALU.mult).then_inc(s["r_step"], 1)
                dve.wait_ge(s["r_step"], 2 * n + 3)
                v.tensor_scalar(ms[q][:], ms[q][:], RMS_EPS, None, ALU.add).then_inc(s["ms_done"], 1)
                norm(q, yl[q], x1[q], mean2[q], rstd2[q]).then_inc(s["yl_done"], 1)

            def a_xn(n, q):
                dve.wait_ge(s["rms_done"], n + 1)
                dve.wait_ge(s["yl_done"], n + 1)
                dve.wait_ge(xn_out[q], i * 8 + CREDIT)
                for t in range(G):
                    last = v.tensor_scalar(xn[q][:, t, :], yl[q][:, t, :], rms[q][:, t:t + 1], None, ALU.mult)
                last.then_inc(s["xn_done"], 1)

            with dve.Fori(0, B - 1, 2) as i:
                for stage in (a_stats, a_norm, a_mask, a_soft, a_res, a_y, a_xn):
                    for q in range(2):
                        stage(i + q, q)

            steps = [1 + 2 * B]

            def step(ins):
                ins.then_inc(s["r_step"], 1)
                steps[0] += 1
                dve.wait_ge(s["r_step"], steps[0])

            def wide(a, n):
                return a.rearrange("p (t o) -> p t o", o=1).to_broadcast([P, a.shape[1], n])

            dve.wait_ge(s["rt_done"], B)
            step(v.tensor_copy(sc[:], route_bank[:, 0:TILES * E].rearrange("p (t e) -> p t e", e=E)))
            for src, top, score_eq, pick, one_hot in ((sc, top1, eq, pick1, hot1), (sc2, top2, eq, pick2, hot2)):
                step(v.tensor_reduce(top[:], src[:], axis=AX.X, op=ALU.max))
                step(v.tensor_tensor(score_eq[:], src[:], wide(top[:], E), ALU.is_equal))
                step(v.tensor_tensor(score_eq[:], score_eq[:], first_w, ALU.mult))
                step(v.tensor_reduce(pick[:], score_eq[:], axis=AX.X, op=ALU.max))
                step(v.tensor_tensor(one_hot[:], first_w, wide(pick[:], E), ALU.is_equal))
                if src is sc:
                    step(v.tensor_scalar(big1[:], hot1[:], -FREE, None, ALU.mult))
                    step(v.tensor_tensor(sc2[:], big1[:], sc[:], ALU.add))
            v.tensor_tensor(hot[:], hot1[:], hot2[:], ALU.add).then_inc(s["hot_done"], 1)
            step(v.tensor_tensor(dist[:], sc[:], wide(top1[:], E), ALU.subtract))
            v.tensor_tensor(top2[:], top2[:], top1[:], ALU.subtract).then_inc(s["dist_done"], 1)
            dve.wait_ge(s["prefix_mm"], 1)
            v.tensor_copy(counts[:], banks[1][:, 0:P]).then_inc(s["counts_done"], 1)
            dve.wait_ge(s["totals_mm"], 1)
            totals = banks[2][:, 0:E].rearrange("p (e o) -> p e o", o=1).to_broadcast([P, E, T // P])
            steps_wide = step_no.rearrange("p (o c) -> p o c", o=1).to_broadcast([P, E, T // P])
            step(v.tensor_tensor(n_gt[:], totals, steps_wide, ALU.is_gt))
            step(v.tensor_reduce(n_blocks[:], n_gt[:], axis=AX.X, op=ALU.add))
            step(v.tensor_tensor(tri[:], lower, n_blocks[:].rearrange("p (o f) -> p o f", o=1)
                                 .to_broadcast([P, E, E]), ALU.mult))
            step(v.tensor_reduce(start_blk[:], tri[:], axis=AX.X, op=ALU.add))
            step(v.tensor_scalar(start_pos[:], start_blk[:], float(P), None, ALU.mult))
            step(v.tensor_tensor(pos_e[:], banks[0][:, 0:TILES * E].rearrange("p (t e) -> p t e", e=E),
                                 start_pos[:].rearrange("p (o e) -> p o e", o=1).to_broadcast([P, TILES, E]),
                                 ALU.add))
            v.tensor_tensor(pos_m[:, 0], pos_e[:], hot1[:], ALU.mult)
            step(v.tensor_tensor(pos_m[:, 1], pos_e[:], hot2[:], ALU.mult))
            step(v.tensor_reduce(pos[:], pos_m[:].rearrange("p k t e -> p (k t) e"), axis=AX.X, op=ALU.add))
            step(v.tensor_copy(pos_i[:], pos[:]))
            v.tensor_scalar(blk_i[:], pos_i[:], 7, None, ALU.logical_shift_right)
            step(v.tensor_scalar(row_i[:], pos_i[:], P - 1, None, ALU.bitwise_and))
            v.tensor_copy(blk_f[:], blk_i[:])
            step(v.tensor_copy(row_f[:], row_i[:]))
            step(v.tensor_tensor(in_block[:], block_no.rearrange("p (o b) -> p o b", o=1)
                                 .to_broadcast([P, K * TILES, BLOCKS]), wide(blk_f[:], BLOCKS), ALU.is_equal))
            for c in range(K * TILES):
                v.tensor_scalar(in_row[:, c, :], iota, row_f[:, c:c + 1], pair_no[:, c:c + 1],
                                ALU.is_equal, ALU.mult).then_inc(s["inrow_done"], 1)
            step(v.tensor_tensor(end_blk[:], start_blk[:], n_blocks[:], ALU.add))
            step(v.tensor_tensor(past[:], end_blk[0:1, :].rearrange("p (o e) -> p o e", o=1)
                                 .to_broadcast([1, BLOCKS, E]), block_no[0:1, :].rearrange("p (b o) -> p b o", o=1)
                                 .to_broadcast([1, BLOCKS, E]), ALU.is_le))
            step(v.tensor_reduce(expert_f[:], past[:], axis=AX.X, op=ALU.add))
            v.tensor_scalar(expert[:], expert_f[:], float(E - 1), None, ALU.min).then_inc(s["expert_done"], 1)
            dve.wait_ge(s["inv_mm"], 1)
            slot = banks[3][:, 0:BLOCKS]
            step(v.tensor_scalar(pair_f[:], slot, -1.0, 0.0, ALU.add, ALU.max))
            step(v.tensor_scalar(second[:], pair_f[:], float(T), -float(T), ALU.is_ge, ALU.mult))
            v.tensor_tensor(src_row[:], pair_f[:], second[:], ALU.add).then_inc(s["src_done"], 1)
            step(v.tensor_scalar(empty[:], slot, 0.0, None, ALU.is_equal))
            step(v.tensor_tensor(spare[:], empty[:], spare_row, ALU.mult))
            v.tensor_tensor(dst_row[:], pair_f[:], spare[:], ALU.add).then_inc(s["dst_done"], 1)
            dve.wait_ge(s["ex_done"], 1)
            step(v.tensor_reduce(den[:], dist[:], axis=AX.X, op=ALU.add))
            step(v.reciprocal(c_rec[:], den[:]))
            step(v.tensor_scalar(weight[:, :, 0], c_rec[:], 0.5, None, ALU.mult))
            step(v.tensor_tensor(weight[:, :, 1], weight[:, :, 0], top2[:], ALU.mult))

            gate = [banks[0], banks[1]]
            val = [banks[2], banks[3]]
            y_bank = banks[7]

            def silu(b, par):
                dve.wait_ge(s["b_th"], b + 1)
                v.scalar_tensor_tensor(gs[par][:], th[par][:], 1.0, gate[par][:, 0:H], ALU.add, ALU.mult
                                       ).then_inc(s["b_gs"], 1)
                dve.wait_ge(s["b_gs"], b + 1)
                v.tensor_tensor(hid[par][:, 0:H], gs[par][:], val[par][:, 0:H], ALU.mult
                                ).then_inc(s["b_hid"], 1)

            def move_y(b, m):
                dve.wait_ge(s["b_dn"], b + 1)
                dve.wait_ge(s["ys_free"], b + 1)
                v.tensor_copy(ys[m][:], y_bank[:, 0:D]).then_inc(s["b_y"], 1)

            dve.wait_ge(s["zeroed"], 1)
            silu(0, 0)
            silu(1, 1)
            with dve.Fori(2, BLOCKS - RING, RING) as i:
                for j in range(RING):
                    move_y(i + j - 2, j)
                    silu(i + j, j % 2)
            b = BLOCKS - 1
            move_y(b - 2, (b - 2) % RING)
            silu(b, b % 2)
            for c in (b - 1, b):
                move_y(c, c % RING)

            attn, mix = [banks[2], banks[3]], [banks[6], banks[7]]

            def c_stats(n, q):
                dve.wait_ge(s["c_x2"], n + 1)
                stats_of(n, q, x2[q], mean[q], ("c_st", "c_ve"))

            def c_norm(n, q):
                dve.wait_ge(s["c_rstd"], n + 1)
                norm(q, xh[q], x2[q], mean[q], rstd[q]).then_inc(s["c_xh"], 1)

            def c_max(n, q):
                dve.wait_ge(s["c_sc"], n + 1)
                v.tensor_reduce(nmax[q][:], attn[q][:, 0:G * J].rearrange("p (t j) -> p t j", j=J), axis=AX.X,
                                op=ALU.max, negate=True).then_inc(s["c_max"], 1)

            def c_res(n, q):
                dve.wait_ge(s["c_exp"], n + 1)
                v.reciprocal(rinv[q][:], rsum[q][:]).then_inc(s["c_rinv"], 1)
                dve.wait_ge(s["c_rinv"], n + 1)
                dve.wait_ge(s["c_pv"], n + 1)
                for t in range(G):
                    last = v.scalar_tensor_tensor(x3[q][:, t, :], mix[q][:, t * D:(t + 1) * D], rinv[q][:, t:t + 1],
                                                  x2[q][:, t, :], ALU.mult, ALU.add)
                last.then_inc(s["c_x3"], 1)
                dve.wait_ge(s["c_x3"], n + 1)
                stats_of(n, q, x3[q], mean2[q], ("c_st4", "c_ve4"))

            def c_z(n, q):
                dve.wait_ge(s["c_rstd4"], n + 1)
                norm(q, xh[q], x3[q], mean2[q], rstd2[q]).then_inc(s["c_z"], 1)

            def c_mix(n, q):
                dve.wait_ge(s["c_dz"], n + 1)
                v.scalar_tensor_tensor(xk[q][:], dz[q][:], mu_k_sb[:], xt[q][:, 0:S], ALU.mult, ALU.add
                                       ).then_inc(s["c_xk"], 1)
                v.scalar_tensor_tensor(xr[q][:], dz[q][:], mu_r_sb[:], xt[q][:, 0:S], ALU.mult, ALU.add
                                       ).then_inc(s["c_xr"], 1)

            def c_square(n, q):
                dve.wait_ge(s["c_rk"], n + 1)
                v.tensor_tensor(ka[q][:], rk[q][:], rk[q][:], ALU.mult).then_inc(s["c_ka"], 1)

            def c_out(n, q):
                dve.wait_ge(s["c_tg"], n + 1)
                dve.wait_ge(s["c_kv"], n + 1)
                v.scalar_tensor_tensor(wv[q][:], tg[q][:], 1.0, mix[q][:], ALU.add, ALU.mult
                                       ).then_inc(s["c_wv"], 1)
                dve.wait_ge(s["c_wv"], n + 1)
                dve.wait_ge(res_out[q], i * 8 + CREDIT)
                v.scalar_tensor_tensor(res[q][:], wv[q][:], 0.5, x3[q][:].rearrange("p t d -> p (t d)"),
                                       ALU.mult, ALU.add).then_inc(s["c_res"], 1)

            with dve.Fori(0, B - 1, 2) as i:
                for stage in (c_stats, c_norm, c_max, c_res, c_z, c_mix, c_square, c_out):
                    for q in range(2):
                        stage(i + q, q)


def shape_constants():
    c = np.zeros((P, C_ALL), np.float32)
    p = np.arange(P)
    c[:, C_IDENT:C_IDENT + P] = np.eye(P)
    c[:, C_IOTA:C_IOTA + P] = p
    c[:, C_FIRST:C_LOWER] = np.tile(E - np.arange(E), TILES)
    c[:, C_LOWER:C_BLOCK] = np.tril(np.ones((E, E)), -1).reshape(-1)
    c[:, C_BLOCK:C_SPARE] = np.arange(BLOCKS)
    c[:, C_SPARE:C_PAIR] = PAIRS + np.arange(BLOCKS) * P + p[:, None]
    c[:, C_PAIR:C_STEP] = 1 + np.arange(K * TILES) * P + p[:, None]
    c[:, C_STEP:C_ALL] = np.arange(T // P) * P
    m = np.zeros((P, M_ALL), np.float16)
    tile_of, expert_of = np.divmod(np.arange(TILES * E), E)
    m[:, M_BEFORE:M_ONES] = p[:, None] < p
    m[:, M_ONES:M_EARLIER] = 1
    m[:, M_EARLIER:M_SAME] = (expert_of[:, None] == expert_of) & (tile_of[:, None] < tile_of)
    m[:, M_SAME:M_ALL] = expert_of[:, None] == np.arange(E)
    return c, m


def kernel(**inputs):
    import concourse.bacc as bacc
    from concourse.bass_utils import run_bass_kernel_spmd

    a = {k: np.asarray(v) for k, v in inputs.items()}
    consts, zero_ones = shape_constants()
    mask = a["mask_1xSxS2_bk0"].reshape(G, P, J).transpose(1, 0, 2)
    arrays = {
        "x": a["x"].reshape(T, D),
        "ctx": a["ctx_1024"].transpose(1, 0, 2),
        "ctx_t": a["ctx_1024"].reshape(B * J, D).T,
        "attn_mask": mask,
        "row_mask": a["mask_BxS2_if1"].reshape(1, B * J),
        "wi": a["L0_xattn_wi"],
        "wi_t": a["L0_xattn_wi"].T,
        "norm_scale": a["L0_ffn_norm_scale"].reshape(D, 1),
        "router_t": a["L0_ffn_w_router"].T,
        "up_t": a["L0_ffn_w_up"].transpose(2, 0, 1),
        "down_t": a["L0_ffn_w_down"].transpose(2, 0, 1),
        "w1_t": a["L1_xattn_W"].T,
        "diagonal": a["L1_xattn_diagonal"].reshape(D, 1),
        "wr_t": a["L1_ffn_W_r"].T,
        "wk_t": a["L1_ffn_W_k"].T,
        "wv_t": a["L1_ffn_W_v"].T,
        "mu_r": a["L1_ffn_mu_r"].reshape(D, 1),
        "mu_k": a["L1_ffn_mu_k"].reshape(D, 1),
        "consts": consts,
        "zero_ones": zero_ones,
    }
    arrays = {k: np.ascontiguousarray(v) for k, v in arrays.items()}
    nc = bacc.Bacc("TRN2", target_bir_lowering=False, num_devices=1)
    aps = [nc.dram_tensor(f"in_{k}", v.shape, mybir.dt.from_np(v.dtype), kind="ExternalInput").ap()
           for k, v in arrays.items()]
    out = nc.dram_tensor("out_rows", (T, D), F32, kind="ExternalOutput").ap()
    build(nc, *aps, out)
    r = run_bass_kernel_spmd(nc, [{f"in_{k}": v for k, v in arrays.items()}], core_ids=[0])
    return r.results[0]["out_rows"].reshape(B, S, D)
```

```python
from contextlib import ExitStack

import numpy as np
import concourse.bass as bass
from concourse import mybir

F32 = mybir.dt.float32
F16 = mybir.dt.float16
I32 = mybir.dt.int32
U8 = mybir.dt.uint8
ALU = mybir.AluOpType
ACT = mybir.ActivationFunctionType
AX = mybir.AxisListType

P = 128
B, S, D = 4, 512, 128
J = 77
E, H = 8, 352
K = 2
T = B * S
TILES = T // P
G = S // P
PAIRS = K * T
BLOCKS = (PAIRS + E * (P - 1)) // P
HC = (H + P - 1) // P
HP = HC * P
H_LAST = H - (HC - 1) * P
SLOTS = BLOCKS * P
RING = 4
LAG0, LAG1 = 4.1, 5.5
LAG = 2
LN_EPS, RMS_EPS = 1e-5, 1e-6
MASKED = -1e10
FREE = 3.0e38

C_IDENT = 0
C_FIRST = C_IDENT + P
C_LOWER = C_FIRST + TILES * E
C_BLOCK = C_LOWER + E * E
C_SPARE = C_BLOCK + BLOCKS
C_STEP = C_SPARE + BLOCKS
C_LANE = C_STEP + T // P
C_ALL = C_LANE + 1
COLS = K * TILES
M_BEFORE = 0
M_ONES = M_BEFORE + P
M_EARLIER = M_ONES + P
M_SAME = M_EARLIER + TILES * E
M_BLOCK = M_SAME + E
M_COL = M_BLOCK + BLOCKS * COLS
M_ALL = M_COL + COLS
A_WI = 0
A_WI_T = A_WI + D
A_CTX_T = A_WI_T + D
A_ALL = A_CTX_T + B * J
W_W1 = 0
W_WR = W_W1 + D
W_WK = W_WR + D
W_WV = W_WK + D
W_ROUTER = W_WV + D
W_SCALE = W_ROUTER + E
W_DIAG = W_SCALE + 1
W_MU_R = W_DIAG + 1
W_MU_K = W_MU_R + 1
W_ALL = W_MU_K + 1


def build(nc, x, ctx, attn_mask, row_mask, keys, weights, up_t, down_t, consts, small, row_no, out):
    with ExitStack() as stack:
        def sb(name, shape, dt=F32):
            return stack.enter_context(nc.sbuf_tensor(name, shape, dt))

        def each(name, shape, dt=F32, n=B):
            return [sb(f"{name}{g}", shape, dt) for g in range(n)]

        def sem(name):
            return stack.enter_context(nc.semaphore(name))

        xn_dram = nc.dram_tensor("xn_rows", [T, D], F32).ap()
        y_dram = nc.dram_tensor("y_rows", [PAIRS + SLOTS, D], F32).ap()

        banks = [stack.enter_context(nc.psum_tensor(f"bank{n}", [P, 512], F32)) for n in range(8)]

        cst = sb("cst", [P, C_ALL])
        m16 = sb("m16", [P, M_ALL], F16)
        row_sb = sb("row_sb", [P, P, COLS], F16)
        ident = cst[:, C_IDENT:C_FIRST]
        first_w = cst[:, C_FIRST:C_LOWER].rearrange("p (t e) -> p t e", e=E)
        lower = cst[:, C_LOWER:C_BLOCK].rearrange("p (e f) -> p e f", f=E)
        block_at = cst[:, C_BLOCK:C_SPARE]
        spare_row = cst[:, C_SPARE:C_STEP]
        step_no = cst[:, C_STEP:C_LANE]
        lane = cst[:, C_LANE:C_ALL]
        block_no = m16[:, M_BLOCK:M_COL].rearrange("p (b c) -> p b c", c=COLS)
        col_no = m16[:, M_COL:M_ALL]
        ctx_sb = sb("ctx_sb", [J, B, D])
        mask_sb = sb("mask_sb", [P, G, J], U8)
        row_mask_sb = sb("row_mask_sb", [1, B * J], I32)
        keys_sb = sb("keys_sb", [P, A_ALL])
        wi_sb, wi_t_sb, ctx_t_sb = (keys_sb[:, a:b] for a, b in (
            (A_WI, A_WI_T), (A_WI_T, A_CTX_T), (A_CTX_T, A_ALL)))
        weights_sb = sb("weights_sb", [P, W_ALL])
        w1_sb, wr_sb, wk_sb, wv_sb, router_sb, scale_sb, diag_sb, mu_r_sb, mu_k_sb = (
            weights_sb[:, a:b] for a, b in (
                (W_W1, W_WR), (W_WR, W_WK), (W_WK, W_WV), (W_WV, W_ROUTER), (W_ROUTER, W_SCALE),
                (W_SCALE, W_DIAG), (W_DIAG, W_MU_R), (W_MU_R, W_MU_K), (W_MU_K, W_ALL)))
        up_sb = sb("up_sb", [P, E, 2 * H])
        down_sb = sb("down_sb", [P, HC, E, D])
        ones_g = sb("ones_g", [P, G])
        power = sb("power", [P, G])

        kt0 = sb("kt0", [P, B * J])
        qs_rhs = sb("qs_rhs", [P, B, D + J])
        v0 = sb("v0", [J, B, D])
        cap = sb("cap", [P, G, J])
        router_s = sb("router_s", [P, E])
        k1 = sb("k1", [P, B, J])
        add1 = sb("add1", [1, B, G, J])
        add1_b = sb("add1_b", [1, B * J])
        ones_row = sb("ones_row", [1, P])
        one_mu = sb("one_mu", [P, 1])
        wr_now = sb("wr_now", [P, D])
        wr_prev = sb("wr_prev", [P, D])
        wv_half = sb("wv_half", [P, D])

        xg = each("xg", [P, G, D])
        stats = each("stats", [P, G, 6])
        mv = each("mv", [P, G, 2])
        shift = each("shift", [P, G])
        ve = each("ve", [P, 2, G])
        rstd = each("rstd", [P, 2, G])
        gain = each("gain", [P, G])
        offset = each("offset", [P, G])
        xh = each("xh", [P, G, D])
        xt = each("xt", [P, S + 1])
        sm = each("sm", [P, G, J])
        nmax = each("nmax", [P, G])
        pr = each("pr", [P, G, J])
        rsum = each("rsum", [P, G])
        rinv = each("rinv", [P, G])
        pt = each("pt", [J, S])
        x1 = each("x1", [P, G, D])
        xn = each("xn", [P, G, D])
        skip = each("skip", [P, G, D])
        yb = each("yb", [P, K, G, D], n=2)
        xk = each("xk", [P, S], n=2)
        rk = each("rk", [P, S], n=2)
        dz = each("dz", [P, S], n=2)

        def route(name, shape=(P, TILES, E), dt=F32):
            return sb(name, list(shape), dt)

        sc, eq, sc2, dist = (route(n) for n in ("sc", "eq", "sc2", "dist"))
        top1, top2, pick1, pick2, den, c_rec = (route(n, (P, TILES)) for n in (
            "top1", "top2", "pick1", "pick2", "den", "c_rec"))
        weight = route("weight", (P, K, TILES))
        hot = sb("hot", [P, K, TILES, E])
        hot16 = route("hot16", dt=F16)
        counts = sb("counts", [P, P], F16)
        n_gt = sb("n_gt", [P, E, T // P])
        n_blocks = sb("n_blocks", [P, E])
        tri = sb("tri", [P, E, E])
        start_pos = sb("start_pos", [P, E])
        end_pos = sb("end_pos", [P, E])
        pos_e = route("pos_e")
        pos_m = sb("pos_m", [P, K, TILES, E])
        pos = sb("pos", [P, COLS])
        pos_i = sb("pos_i", [P, COLS], I32)
        blk_i = sb("blk_i", [P, COLS], I32)
        row_i = sb("row_i", [P, COLS], I32)
        blk_h = sb("blk_h", [P, COLS], F16)
        row_h = sb("row_h", [P, COLS], F16)
        in_block = sb("in_block", [P, BLOCKS, COLS], F16)
        marks = sb("marks", [P, 2, BLOCKS, COLS], F16)
        in_row = sb("in_row", [P, P, COLS], F16)
        past = sb("past", [1, BLOCKS, E])
        expert_f = sb("expert_f", [1, BLOCKS])
        expert = sb("expert", [1, BLOCKS], I32)
        lane_f = sb("lane_f", [P, BLOCKS])
        pair_f = sb("pair_f", [P, BLOCKS])
        second = sb("second", [P, BLOCKS])
        spare = sb("spare", [P, BLOCKS])
        src_row = sb("src_row", [P, BLOCKS], I32)
        dst_row = sb("dst_row", [P, BLOCKS], I32)

        rows = each("rows", [P, D], n=RING)
        rows_t = each("rows_t", [P, P], n=2)
        th = each("th", [P, H], n=2)
        gs = each("gs", [P, H], n=2)
        hid = each("hid", [P, HP], n=2)
        hid_t = each("hid_t", [P, HP], n=2)
        ys = each("ys", [P, D], n=RING)

        NAMES = """keys_in weights_in ctx_in consts_in small_in row_no_in mask_in experts_in zeroed
            kt0_mm kt0_sb qs_mm v0_mm k1_mm wi_copied cap_done setup_dve setup_act setup_step
            st ve rstd shift xh xt_mm xt qs sm max exp rinv pr pt_mm pt pv x1 ve2 rstd_x rstd_y
            shift2 xn xn_mm xnt rt sc_sb pool_step skip
            step hot_done prefix_mm counts_done totals_mm dist_done ex_done inrow_done
            inv_mm src_done dst_done expert_done weight_done
            b_xt_mm b_xt b_up b_th b_gs b_hid b_ht_mm b_ht b_dn b_y ys_free
            c_step c_x2 c_ve c_rstd c_shift c_xh c_xt_mm c_xt c_rt_mm c_rt c_sc c_max c_exp c_rinv
            c_pt_mm c_pt c_pv c_x3 c_ve4 c_rstd4 c_z c_zt_mm c_zt c_dz c_xk c_k c_r c_rk c_ka
            c_tg c_kv c_wv c_res""".split()
        s = {n: sem(n) for n in NAMES}
        x_in = [sem(f"x_in{n}") for n in range(B)]
        xn_out = sem("xn_out")
        rows_in = [sem(f"rows_in{m}") for m in range(RING)]
        ys_out = [sem(f"ys_out{m}") for m in range(RING)]
        yb_in = [sem(f"yb_in{n}") for n in range(B)]
        res_out = sem("res_out")

        def scores0(n, half):
            return banks[2 * (n % 2) + half][:, 0:2 * (D + J)].rearrange("p (t c) -> p t c", t=2)

        xh_bank, pr_bank, xn_bank, route_bank = banks[4], banks[5], banks[6], banks[7]
        gate, val = [banks[0], banks[1]], [banks[2], banks[3]]
        rt_bank, ht_bank, y_bank = banks[4], [banks[5], banks[6]], banks[7]
        c_xh_bank, c_rt_bank, c_at_bank, c_pv_bank, c_z_bank, c_k_bank, c_r_bank, c_kv_bank = banks

        def tiles_in(dram, n):
            return dram[n * S:(n + 1) * S, :].rearrange("(t p) d -> p t d", p=P)

        def staggered(stages, lag):
            return [(f, n) for _, n, f in sorted(
                ((at + lag * n, n, f) for at, f in stages for n in range(B)), key=lambda x: x[:2])]

        block = stack.enter_context(nc.Block())

        @block.sync
        def _(sp):
            sp.dma_start(keys_sb[:], keys).then_inc(s["keys_in"], 16)
            sp.dma_start(xg[0][:], tiles_in(x, 0)).then_inc(x_in[0], 16)
            sp.dma_start(mask_sb[:], attn_mask).then_inc(s["mask_in"], 16)
            sp.dma_start(weights_sb[:], weights).then_inc(s["weights_in"], 16)
            sp.dma_start(xg[1][:], tiles_in(x, 1)).then_inc(x_in[1], 16)
            sp.dma_start(row_mask_sb[:], row_mask).then_inc(s["mask_in"], 16)
            sp.dma_start(cst[:], consts).then_inc(s["consts_in"], 16)
            for n in range(2, B):
                sp.dma_start(xg[n][:], tiles_in(x, n)).then_inc(x_in[n], 16)
            sp.dma_start(m16[:], small).then_inc(s["small_in"], 16)
            sp.dma_start(row_sb[:].rearrange("p r c -> p (r c)"), row_no).then_inc(s["row_no_in"], 16)
            sp.dma_start(ctx_sb[:], ctx).then_inc(s["ctx_in"], 16)
            for e in range(0, E, 2):
                sp.dma_start(up_sb[:, e:e + 2], up_t[:, e:e + 2]).then_inc(s["experts_in"], 16)
            sp.dma_start(down_sb[:, 0:HC - 1], down_t[0:(HC - 1) * P].rearrange("(c p) e d -> p c e d", p=P)
                         ).then_inc(s["experts_in"], 16)
            sp.dma_start(down_sb[0:H_LAST, HC - 1], down_t[(HC - 1) * P:H]).then_inc(s["experts_in"], 16)
            for n in range(B):
                sp.wait_ge(s["xn"], n + 1)
                sp.dma_start(tiles_in(xn_dram, n), xn[n][:]).then_inc(xn_out, 16)
            for m in range(RING):
                sp.wait_ge(ys_out[m], 16 * ((BLOCKS - m + RING - 1) // RING))
            for n in range(B):
                if n >= 2:
                    sp.wait_ge(s["c_x2"], n - 1)
                for k in range(K):
                    sp.dma_start(yb[n % 2][:, k], tiles_in(y_dram[k * T:(k + 1) * T, :], n)
                                 ).then_inc(yb_in[n], 16)
            for n in range(B):
                sp.wait_ge(s["c_res"], n + 1)
                sp.dma_start(tiles_in(out, n), xh[n][:]).then_inc(res_out, 16)
            sp.wait_ge(res_out, 16 * B)
            sp.wait_ge(xn_out, 16 * B)

        @block.gpsimd
        def _(pool):
            nc.gpsimd.memset(power[:], -0.5)
            nc.gpsimd.memset(ones_g[:], 1.0)
            for m in range(2):
                nc.gpsimd.memset(hid[m][:, H:HP], 0.0)
            for n in range(B):
                nc.gpsimd.memset(xt[n][:, 0:1], 0.0)
            nc.gpsimd.memset(ones_row[:], 1.0).then_inc(s["zeroed"], 1)
            pool.wait_ge(s["zeroed"], 1)
            pool.sem_inc(s["ys_free"], RING)

            def root(n, row, ready, signal):
                pool.wait_ge(s[ready], n + 1)
                nc.gpsimd.tensor_tensor(rstd[n][:, row], ve[n][:, row], power[:], ALU.pow
                                        ).then_inc(s[signal], 1)

            def rstd0(n):
                root(n, 0, "ve", "rstd")

            def rstd_xn(n):
                root(n, 1, "ve2", "rstd_x")

            def rstd_y(n):
                root(n, 0, "ve2", "rstd_y")

            def skip0(n):
                pool.wait_ge(s["rstd_y"], n + 1)
                nc.gpsimd.tensor_tensor(gain[n][:], rstd[n][:, 0], ones_g[:], ALU.add)
                nc.gpsimd.tensor_tensor(offset[n][:], mv[n][:, :, 0], rstd[n][:, 0], ALU.mult
                                        ).then_inc(s["pool_step"], 1)
                pool.wait_ge(s["pool_step"], 2 * n + 1)
                nc.gpsimd.tensor_tensor(skip[n][:], x1[n][:], gain[n][:].rearrange("p (t o) -> p t o", o=1)
                                        .to_broadcast([P, G, D]), ALU.mult).then_inc(s["pool_step"], 1)
                pool.wait_ge(s["pool_step"], 2 * n + 2)
                nc.gpsimd.tensor_tensor(skip[n][:], skip[n][:], offset[n][:].rearrange("p (t o) -> p t o", o=1)
                                        .to_broadcast([P, G, D]), ALU.subtract).then_inc(s["skip"], 1)

            for stage, n in staggered(((7.1, rstd0), (23.1, rstd_xn), (24.6, rstd_y), (25.1, skip0)), LAG0):
                stage(n)

            def gather(b):
                if b >= RING:
                    pool.wait_ge(s["b_xt_mm"], b - RING + 1)
                pool.indirect_dma_start(
                    out=rows[b % RING][:], out_offset=None, in_=xn_dram,
                    in_offset=bass.IndirectOffsetOnAxis(ap=src_row[:, b:b + 1], axis=0),
                ).then_inc(rows_in[b % RING], 16)

            def scatter(b):
                if b >= LAG:
                    pool.wait_ge(ys_out[(b - LAG) % RING], 16 * ((b - LAG) // RING + 1))
                    pool.sem_inc(s["ys_free"], 1)
                pool.wait_ge(s["b_y"], 1 + b + 1)
                pool.indirect_dma_start(
                    out=y_dram, out_offset=bass.IndirectOffsetOnAxis(ap=dst_row[:, b:b + 1], axis=0),
                    in_=ys[b % RING][:], in_offset=None,
                ).then_inc(ys_out[b % RING], 16)

            pool.wait_ge(xn_out, 16 * B)
            pool.wait_ge(s["src_done"], 1)
            for b in range(RING):
                gather(b)
            pool.wait_ge(s["dst_done"], 1)
            for b in range(RING, BLOCKS):
                gather(b)
                if b - RING - 2 >= 0:
                    scatter(b - RING - 2)
            for b in range(BLOCKS - RING - 2, BLOCKS):
                scatter(b)

            def rstd3(n):
                root(n, 0, "c_ve", "c_rstd")

            def rstd4(n):
                root(n, 0, "c_ve4", "c_rstd4")

            def before(n):
                pool.wait_ge(s["c_zt"], n + 1)
                if n >= 2:
                    pool.wait_ge(s["c_xk"], n - 1)
                nc.gpsimd.tensor_tensor(dz[n % 2][:], xt[n][:, 1:S + 1], xt[n][:, 0:S], ALU.subtract
                                        ).then_inc(s["c_dz"], 1)

            def add_mix(n):
                pool.wait_ge(s["c_wv"], n + 1)
                nc.gpsimd.tensor_tensor(xh[n][:], xh[n][:], x1[n][:], ALU.add).then_inc(s["c_res"], 1)

            for stage, n in staggered(((5.9, rstd3), (20, rstd4), (23.3, before), (38.1, add_mix)), LAG1):
                stage(n)

        @block.tensor
        def _(pe):
            mm = nc.tensor.matmul
            pe.wait_ge(s["keys_in"], 16)
            mm(banks[0][:, 0:B * J], wi_sb, ctx_t_sb, start=True, stop=True).then_inc(s["kt0_mm"], 1)
            for b in range(B):
                last = mm(banks[1][0:J, b * D:(b + 1) * D], ctx_t_sb[:, b * J:(b + 1) * J], wi_sb,
                          start=True, stop=True)
            last.then_inc(s["v0_mm"], 1)
            pe.wait_ge(s["kt0_sb"], 1)
            mm(banks[2][:, 0:B * J], wi_t_sb, kt0[:], start=True, stop=True).then_inc(s["qs_mm"], 1)
            pe.wait_ge(s["weights_in"], 16)
            mm(pr_bank[:, 0:B * J], w1_sb, ctx_t_sb, start=True, stop=True).then_inc(s["k1_mm"], 1)
            pe.wait_ge(s["consts_in"], 16)

            def transpose_group(n, bank, src, ready, signal, rows_out=P):
                pe.wait_ge(s[ready], n + 1)
                for t in range(G):
                    last = nc.tensor.transpose(bank[0:rows_out, t * P:(t + 1) * P], src[n][:, t, :], ident)
                last.then_inc(s[signal], 1)

            def tile_t(buf, n, t, back=0):
                return buf[n][:, 1 + t * P - back:1 + (t + 1) * P - back]

            def t_xh(n):
                if n:
                    pe.wait_ge(s["xt"], n)
                transpose_group(n, xh_bank, xh, "xh", "xt_mm")

            def qs(n):
                pe.wait_ge(s["xt"], n + 1)
                if n == 0:
                    pe.wait_ge(s["setup_act"], 1)
                    pe.wait_ge(s["wi_copied"], 1)
                if n >= 2:
                    pe.wait_ge(s["x1"], n - 1)
                for t in range(G):
                    last = mm(scores0(n, t // 2)[:, t % 2, :], tile_t(xt, n, t), qs_rhs[:, n, :],
                              start=(t % 2 == 0), stop=(t % 2 == 1), skip_group_check=True)
                last.then_inc(s["qs"], 1)

            def t_pr(n):
                if n:
                    pe.wait_ge(s["pt"], n)
                else:
                    pe.wait_ge(s["setup_dve"], 1)
                transpose_group(n, pr_bank, pr, "pr", "pt_mm", J)

            def pv(n):
                pe.wait_ge(s["pt"], n + 1)
                for t in range(G):
                    last = mm(scores0(n, t // 2)[:, t % 2, 0:D], pt[n][:, t * P:(t + 1) * P], v0[:, n, :],
                              start=False, stop=True, skip_group_check=True)
                last.then_inc(s["pv"], 1)

            def t_xn(n):
                if n:
                    pe.wait_ge(s["xnt"], n)
                transpose_group(n, xn_bank, xn, "xn", "xn_mm")

            def router(n):
                pe.wait_ge(s["xnt"], n + 1)
                if n:
                    pe.wait_ge(s["sc_sb"], n)
                for t in range(G):
                    last = mm(route_bank[:, t * E:(t + 1) * E], tile_t(xt, n, t), router_s[:],
                              start=True, stop=True)
                last.then_inc(s["rt"], 1)

            for stage, n in staggered(((10, t_xh), (11.6, qs), (15.8, t_pr), (18.7, pv), (25.8, t_xn),
                                       (27.6, router)), LAG0):
                stage(n)

            prefix = banks[0][:, 0:TILES * E]
            pe.wait_ge(s["small_in"], 16)
            pe.wait_ge(s["hot_done"], 1)
            hot2d = hot16[:].rearrange("p t e -> p (t e)")
            mm(banks[1][:, 0:P], hot2d, m16[:, M_ONES:M_ONES + P], start=True, stop=True).then_inc(s["prefix_mm"], 1)
            mm(prefix, m16[:, M_BEFORE:M_BEFORE + P], hot2d, start=True, stop=False)
            pe.wait_ge(s["counts_done"], 1)
            mm(banks[2][:, 0:E], counts[:], m16[:, M_SAME:M_SAME + E], start=True, stop=True)
            mm(prefix, counts[:], m16[:, M_EARLIER:M_EARLIER + TILES * E], start=False, stop=True
               ).then_inc(s["totals_mm"], 1)
            for c in range(COLS):
                if c % TILES == 0:
                    pe.wait_ge(s["inrow_done"], c // TILES + 1)
                last = mm(banks[3][:, 0:2 * BLOCKS], in_row[:, :, c], marks[:, :, :, c],
                          start=(c == 0), stop=(c == COLS - 1))
            last.then_inc(s["inv_mm"], 1)

            def t_rows(b, m, landed):
                pe.wait_ge(rows_in[m], landed)
                nc.tensor.transpose(rt_bank[:, 0:P], rows[m][:], ident).then_inc(s["b_xt_mm"], 1)

            def expert_of(b):
                return pe.value_load(expert[0:1, bass.ds(b, 1)], min_val=0, max_val=E - 1)

            def up(b, par):
                e = expert_of(b)
                pe.wait_ge(s["b_xt"], b + 1)
                for dst, at in ((gate[par], H), (val[par], 0)):
                    last = mm(dst[:, 0:H], rows_t[par][:],
                              up_sb[:, bass.ds(e, 1), at:at + H].rearrange("p o c -> p (o c)"),
                              start=True, stop=True)
                last.then_inc(s["b_up"], 1)

            def t_hid(b, par):
                pe.wait_ge(s["b_hid"], b + 1)
                for c in range(HC):
                    last = nc.tensor.transpose(ht_bank[par][:, c * P:(c + 1) * P],
                                               hid[par][:, c * P:(c + 1) * P], ident)
                last.then_inc(s["b_ht_mm"], 1)

            def down(b, par):
                e = expert_of(b)
                pe.wait_ge(s["b_ht"], b + 1)
                pe.wait_ge(s["b_y"], 1 + b)
                for c in range(HC):
                    kk = P if c < HC - 1 else H_LAST
                    last = mm(y_bank[:, 0:D], hid_t[par][0:kk, c * P:(c + 1) * P],
                              down_sb[0:kk, c, bass.ds(e, 1), :].rearrange("p o c -> p (o c)"),
                              start=(c == 0), stop=(c == HC - 1))
                last.then_inc(s["b_dn"], 1)

            pe.wait_ge(s["expert_done"], 1)
            pe.wait_ge(s["dst_done"], 1)
            pe.wait_ge(s["experts_in"], 16 * (E // 2 + 2))
            t_rows(0, 0, 16)
            up(0, 0)
            t_rows(1, 1, 16)
            up(1, 1)
            t_rows(2, 2, 16)
            t_hid(0, 0)
            with pe.Fori(2, BLOCKS - RING, RING) as i:
                for j in range(RING):
                    b, m = i + j, (2 + j) % RING
                    up(b, m % 2)
                    t_rows(b + 1, (m + 1) % RING, (i + (j + 1 - (m + 1) % RING)) * 4 + 16)
                    down(b - 2, m % 2)
                    t_hid(b - 1, (m + 1) % 2)
            b = BLOCKS - 1
            up(b, b % 2)
            down(b - 2, b % 2)
            t_hid(b - 1, (b - 1) % 2)
            down(b - 1, (b - 1) % 2)
            t_hid(b, b % 2)
            down(b, b % 2)

            def c_t_xh(n):
                if n:
                    pe.wait_ge(s["c_xt"], n)
                transpose_group(n, c_xh_bank, xh, "c_xh", "c_xt_mm")

            def c_rt(n):
                pe.wait_ge(s["c_xt"], n + 1)
                if n:
                    pe.wait_ge(s["c_rt"], n)
                mm(c_rt_bank[:], w1_sb, xt[n][:, 1:S + 1], start=True, stop=True).then_inc(s["c_rt_mm"], 1)

            def c_scores(n):
                pe.wait_ge(s["c_rt"], n + 1)
                if n:
                    pe.wait_ge(s["c_pt"], n)
                mm(c_at_bank[:, 0:G * J], ones_row[:], add1[:, n, :, :].rearrange("p t j -> p (t j)"),
                   start=True, stop=False, skip_group_check=True)
                for t in range(G):
                    last = mm(c_at_bank[:, t * J:(t + 1) * J], xn[n][:, t, :], k1[:, n, :],
                              start=False, stop=(t == G - 1), skip_group_check=True)
                last.then_inc(s["c_sc"], 1)

            def c_t_pr(n):
                transpose_group(n, c_at_bank, pr, "c_exp", "c_pt_mm", J)

            def c_pv(n):
                pe.wait_ge(s["c_pt"], n + 1)
                if n == 0:
                    pe.wait_ge(s["ctx_in"], 16)
                if n:
                    pe.wait_ge(s["c_x3"], n)
                for t in range(G):
                    last = mm(c_pv_bank[:, t * D:(t + 1) * D], pt[n][:, t * P:(t + 1) * P], ctx_sb[:, n, :],
                              start=True, stop=True)
                last.then_inc(s["c_pv"], 1)

            def c_t_z(n):
                if n:
                    pe.wait_ge(s["c_zt"], n)
                transpose_group(n, c_z_bank, xh, "c_z", "c_zt_mm")

            def c_r(n):
                pe.wait_ge(s["c_zt"], n + 1)
                if n:
                    pe.wait_ge(s["c_tg"], n)
                for t in range(G):
                    mm(c_r_bank[:, t * D:(t + 1) * D], tile_t(xt, n, t), wr_now[:], start=True, stop=False)
                    last = mm(c_r_bank[:, t * D:(t + 1) * D], tile_t(xt, n, t, 1), wr_prev[:],
                              start=False, stop=True)
                last.then_inc(s["c_r"], 1)

            def c_k(n):
                pe.wait_ge(s["c_xk"], n + 1)
                if n:
                    pe.wait_ge(s["c_rk"], n)
                mm(c_k_bank[:], wk_sb, xk[n % 2][:], start=True, stop=True).then_inc(s["c_k"], 1)

            def c_kv(n):
                pe.wait_ge(s["c_ka"], n + 1)
                if n:
                    pe.wait_ge(s["c_wv"], n)
                for t in range(G):
                    last = mm(c_kv_bank[:, t * D:(t + 1) * D], rk[n % 2][:, t * P:(t + 1) * P], wv_half[:],
                              start=True, stop=True)
                last.then_inc(s["c_kv"], 1)

            for stage, n in staggered(((11.1, c_t_xh), (11.6, c_rt), (13.7, c_scores), (16.7, c_t_pr), (17.8, c_pv),
                                       (23.8, c_t_z), (26.8, c_r), (27.8, c_k), (30.9, c_kv)), LAG1):
                stage(n)

        @block.scalar
        def _(act):
            act.wait_ge(s["kt0_mm"], 1)
            nc.scalar.activation(kt0[:], banks[0][:, 0:B * J], ACT.Copy).then_inc(s["kt0_sb"], 1)
            act.wait_ge(s["v0_mm"], 1)
            nc.scalar.activation(v0[:], banks[1][0:J, :].rearrange("p (b d) -> p b d", d=D), ACT.Copy)
            act.wait_ge(s["qs_mm"], 1)
            nc.scalar.activation(qs_rhs[:, :, D:D + J], banks[2][:, 0:B * J].rearrange("p (b j) -> p b j", j=J),
                                 ACT.Copy, scale=float(D) ** -0.5).then_inc(s["setup_act"], 1)
            act.wait_ge(s["zeroed"], 1)

            def move_t(n, bank, ready, signal):
                act.wait_ge(s[ready], n + 1)
                nc.scalar.activation(xt[n][:, 1:S + 1], bank[:], ACT.Copy).then_inc(s[signal], 1)

            def move_pt(n, bank, ready, signal):
                act.wait_ge(s[ready], n + 1)
                nc.scalar.activation(pt[n][:], bank[0:J, :], ACT.Copy).then_inc(s[signal], 1)

            def exps(n, src, ready, signal):
                act.wait_ge(s[ready], n + 1)
                for t in range(G):
                    last = nc.scalar.activation(pr[n][:, t, :], src(t), ACT.Exp, bias=nmax[n][:, t:t + 1],
                                                accum_out=rsum[n][:, t:t + 1])
                last.then_inc(s[signal], 1)

            def norm(n, dst, src, ready, signal, row=0):
                act.wait_ge(s[ready], n + 1)
                for t in range(G):
                    last = nc.scalar.activation(dst[n][:, t, :], src[n][:, t, :], ACT.Identity,
                                                bias=shift[n][:, t:t + 1], scale=rstd[n][:, row, t:t + 1])
                last.then_inc(s[signal], 1)

            def a_norm(n):
                norm(n, xh, xg, "shift", "xh")

            def a_move_xt(n):
                move_t(n, xh_bank, "xt_mm", "xt")

            def a_exp(n):
                exps(n, lambda t: sm[n][:, t, :], "max", "exp")

            def a_move_pt(n):
                move_pt(n, pr_bank, "pt_mm", "pt")

            def a_xn(n):
                norm(n, xn, x1, "shift2", "xn", 1)

            def a_move_xn(n):
                move_t(n, xn_bank, "xn_mm", "xnt")

            for stage, n in staggered(((7.1, a_norm), (10.1, a_move_xt), (14.4, a_exp), (16.2, a_move_pt),
                                       (23.6, a_xn), (26.7, a_move_xn)), LAG0):
                stage(n)

            act.wait_ge(s["dist_done"], 1)
            nc.scalar.activation(dist[:], dist[:], ACT.Exp)
            nc.scalar.activation(top2[:], top2[:], ACT.Exp).then_inc(s["ex_done"], 1)

            def move_rows(b, par):
                act.wait_ge(s["b_xt_mm"], b + 1)
                nc.scalar.activation(rows_t[par][:], rt_bank[:, 0:P], ACT.Copy, scale=scale_sb
                                     ).then_inc(s["b_xt"], 1)

            def tanh_gate(b, par):
                act.wait_ge(s["b_up"], b + 1)
                nc.scalar.activation(th[par][:], gate[par][:, 0:H], ACT.Tanh, scale=0.5).then_inc(s["b_th"], 1)

            def move_hid(b, par):
                act.wait_ge(s["b_ht_mm"], b + 1)
                nc.scalar.activation(hid_t[par][:], ht_bank[par][:, 0:HP], ACT.Copy).then_inc(s["b_ht"], 1)

            move_rows(0, 0)
            tanh_gate(0, 0)
            move_rows(1, 1)
            tanh_gate(1, 1)
            move_rows(2, 0)
            move_hid(0, 0)
            with act.Fori(2, BLOCKS - RING, RING) as i:
                for j in range(RING):
                    b, par = i + j, j % 2
                    tanh_gate(b, par)
                    move_rows(b + 1, 1 - par)
                    move_hid(b - 1, 1 - par)
            b = BLOCKS - 1
            tanh_gate(b, b % 2)
            move_hid(b - 1, (b - 1) % 2)
            move_hid(b, b % 2)

            def c_norm(n):
                norm(n, xh, xg, "c_shift", "c_xh")

            def c_move_xt(n):
                move_t(n, c_xh_bank, "c_xt_mm", "c_xt")

            def c_relu_rt(n):
                act.wait_ge(s["c_rt_mm"], n + 1)
                nc.scalar.activation(xn[n][:].rearrange("p t d -> p (t d)"), c_rt_bank[:], ACT.Relu
                                     ).then_inc(s["c_rt"], 1)

            def c_exp(n):
                exps(n, lambda t: c_at_bank[:, t * J:(t + 1) * J], "c_max", "c_exp")

            def c_move_pt(n):
                move_pt(n, c_at_bank, "c_pt_mm", "c_pt")

            def c_move_zt(n):
                move_t(n, c_z_bank, "c_zt_mm", "c_zt")

            def c_relu_k(n):
                act.wait_ge(s["c_k"], n + 1)
                if n >= 2:
                    act.wait_ge(s["c_kv"], n - 1)
                nc.scalar.activation(rk[n % 2][:], c_k_bank[:], ACT.Relu).then_inc(s["c_rk"], 1)
                act.wait_ge(s["c_rk"], n + 1)
                nc.scalar.activation(rk[n % 2][:], rk[n % 2][:], ACT.Square).then_inc(s["c_ka"], 1)

            def c_tanh(n):
                act.wait_ge(s["c_r"], n + 1)
                nc.scalar.activation(xh[n][:].rearrange("p t d -> p (t d)"), c_r_bank[:], ACT.Tanh, scale=0.5
                                     ).then_inc(s["c_tg"], 1)

            for stage, n in staggered(((9.8, c_norm), (12.4, c_move_xt), (12.9, c_relu_rt), (16.2, c_exp),
                                       (18.3, c_move_pt), (24.1, c_move_zt), (27.9, c_tanh), (29.4, c_relu_k)),
                                      LAG1):
                stage(n)

        @block.vector
        def _(dve):
            v = nc.vector
            dve.sem_inc(s["b_y"], 1)

            dve.wait_ge(s["keys_in"], 16)
            for b in range(B):
                last = v.tensor_copy(qs_rhs[:, b, 0:D], wi_sb)
            last.then_inc(s["wi_copied"], 1)

            def setup_rest():
                dve.wait_ge(s["mask_in"], 32)
                v.tensor_scalar(cap[:], mask_sb[:], FREE, MASKED, ALU.mult, ALU.add).then_inc(s["cap_done"], 1)
                dve.wait_ge(s["weights_in"], 16)
                v.tensor_scalar(router_s[:], router_sb, scale_sb, None, ALU.mult)
                v.tensor_scalar(add1_b[:], row_mask_sb[:], 1e4, -1e4, ALU.mult, ALU.add)
                v.tensor_scalar(one_mu[:], mu_r_sb, -1.0, 1.0, ALU.mult, ALU.add).then_inc(s["setup_step"], 1)
                dve.wait_ge(s["setup_step"], 1)
                v.tensor_copy(add1[:], add1_b[:].rearrange("p (b o j) -> p b o j", b=B, o=1)
                              .to_broadcast([1, B, G, J]))
                v.tensor_scalar(wr_now[:], wr_sb, mu_r_sb, None, ALU.mult)
                v.tensor_scalar(wr_prev[:], wr_sb, one_mu[:], None, ALU.mult)
                v.tensor_scalar(wv_half[:], wv_sb, 0.5, None, ALU.mult)
                dve.wait_ge(s["k1_mm"], 1)
                v.tensor_scalar(k1[:], pr_bank[:, 0:B * J].rearrange("p (b j) -> p b j", j=J), 0.0, diag_sb,
                                ALU.max, ALU.mult).then_inc(s["setup_dve"], 1)

            st_count = [0]

            def st_step(ins):
                ins.then_inc(s["st"], 1)
                st_count[0] += 1
                dve.wait_ge(s["st"], st_count[0])

            def stats_of(n, src, signal, also_xn=False):
                for t in range(G):
                    last = v.bn_stats(stats[n][:, t, :], src[n][:, t, :])
                st_step(last)
                for t in range(G):
                    last = v.bn_aggr(mv[n][:, t, :], stats[n][:, t, :])
                st_step(last)
                if also_xn:
                    v.tensor_scalar(ve[n][:, 1], mv[n][:, :, 1], 1.0 + RMS_EPS, LN_EPS * RMS_EPS, ALU.mult, ALU.add)
                v.tensor_scalar(ve[n][:, 0], mv[n][:, :, 1], LN_EPS, None, ALU.add).then_inc(s[signal], 1)

            def shift_of(n, ready, signal, row=0):
                dve.wait_ge(s[ready], n + 1)
                v.scalar_tensor_tensor(shift[n][:], mv[n][:, :, 0], -1.0, rstd[n][:, row], ALU.mult, ALU.mult
                                       ).then_inc(s[signal], 1)

            def norm(dst, src, n, factor, signal):
                for t in range(G):
                    last = v.tensor_scalar(dst[n][:, t, :], src[n][:, t, :], mv[n][:, t, 0:1],
                                           factor[:, t:t + 1], ALU.subtract, ALU.mult)
                last.then_inc(s[signal], 1)

            def a_stats(n):
                dve.wait_ge(x_in[n], 16)
                stats_of(n, xg, "ve")

            def a_shift(n):
                shift_of(n, "rstd", "shift")

            def a_mask(n):
                dve.wait_ge(s["cap_done"], 1)
                dve.wait_ge(s["qs"], n + 1)
                for h in range(2):
                    last = v.tensor_tensor(sm[n][:, 2 * h:2 * h + 2, :], scores0(n, h)[:, :, D:D + J],
                                           cap[:, 2 * h:2 * h + 2, :], ALU.min)
                last.then_inc(s["sm"], 1)
                dve.wait_ge(s["sm"], n + 1)
                v.tensor_reduce(nmax[n][:], sm[n][:], axis=AX.X, op=ALU.max, negate=True).then_inc(s["max"], 1)

            def a_soft(n):
                dve.wait_ge(s["exp"], n + 1)
                v.reciprocal(rinv[n][:], rsum[n][:]).then_inc(s["rinv"], 1)
                dve.wait_ge(s["rinv"], n + 1)
                v.tensor_tensor(pr[n][:], pr[n][:],
                                rinv[n][:].rearrange("p (t o) -> p t o", o=1).to_broadcast([P, G, J]),
                                ALU.mult).then_inc(s["pr"], 1)

            def a_res(n):
                dve.wait_ge(s["pv"], n + 1)
                for h in range(2):
                    last = v.tensor_tensor(x1[n][:, 2 * h:2 * h + 2, :], scores0(n, h)[:, :, 0:D],
                                           xg[n][:, 2 * h:2 * h + 2, :], ALU.add)
                last.then_inc(s["x1"], 1)

            def a_stats2(n):
                dve.wait_ge(s["x1"], n + 1)
                stats_of(n, x1, "ve2", also_xn=True)

            def a_shift2(n):
                shift_of(n, "rstd_x", "shift2", 1)

            def a_scores(n):
                dve.wait_ge(s["rt"], n + 1)
                v.tensor_copy(sc[:, n * G:(n + 1) * G, :], route_bank[:, 0:G * E].rearrange("p (t e) -> p t e", e=E)
                              ).then_inc(s["sc_sb"], 1)

            for stage, n in staggered(((2.3, a_stats), (6.2, a_shift), (14.3, a_mask), (17.3, a_soft), (19.1, a_res),
                                       (21.9, a_stats2), (22.7, a_shift2), (30.4, a_scores)), LAG0):
                if stage is a_mask and n == 0:
                    setup_rest()
                stage(n)

            steps = [0]

            def step(ins):
                ins.then_inc(s["step"], 1)
                steps[0] += 1
                dve.wait_ge(s["step"], steps[0])

            def wide(a, n):
                return a.rearrange("p (t o) -> p t o", o=1).to_broadcast([P, a.shape[1], n])

            dve.wait_ge(s["sc_sb"], B)
            for k, src, top, pick in ((0, sc, top1, pick1), (1, sc2, top2, pick2)):
                step(v.tensor_reduce(top[:], src[:], axis=AX.X, op=ALU.max))
                step(v.tensor_tensor(eq[:], src[:], wide(top[:], E), ALU.is_equal))
                step(v.tensor_tensor(eq[:], eq[:], first_w, ALU.mult))
                step(v.tensor_reduce(pick[:], eq[:], axis=AX.X, op=ALU.max))
                step(v.tensor_tensor(hot[:, k], first_w, wide(pick[:], E), ALU.is_equal))
                if k == 0:
                    step(v.scalar_tensor_tensor(sc2[:], hot[:, 0], -FREE, sc[:], ALU.mult, ALU.add))
            v.tensor_tensor(hot16[:], hot[:, 0], hot[:, 1], ALU.add).then_inc(s["hot_done"], 1)
            v.tensor_tensor(dist[:], sc[:], wide(top1[:], E), ALU.subtract)
            v.tensor_tensor(top2[:], top2[:], top1[:], ALU.subtract).then_inc(s["dist_done"], 1)
            dve.wait_ge(s["prefix_mm"], 1)
            v.tensor_copy(counts[:], banks[1][:, 0:P]).then_inc(s["counts_done"], 1)
            dve.wait_ge(s["totals_mm"], 1)
            totals = banks[2][:, 0:E].rearrange("p (e o) -> p e o", o=1).to_broadcast([P, E, T // P])
            steps_wide = step_no.rearrange("p (o c) -> p o c", o=1).to_broadcast([P, E, T // P])
            step(v.tensor_tensor(n_gt[:], totals, steps_wide, ALU.is_gt))
            step(v.tensor_reduce(n_blocks[:], n_gt[:], axis=AX.X, op=ALU.add))
            step(v.tensor_tensor(tri[:], lower, n_blocks[:].rearrange("p (o f) -> p o f", o=1)
                                 .to_broadcast([P, E, E]), ALU.mult))
            step(v.tensor_reduce(start_pos[:], tri[:], axis=AX.X, op=ALU.add))
            step(v.tensor_tensor(pos_e[:], banks[0][:, 0:TILES * E].rearrange("p (t e) -> p t e", e=E),
                                 start_pos[:].rearrange("p (o e) -> p o e", o=1).to_broadcast([P, TILES, E]),
                                 ALU.add))
            v.tensor_tensor(pos_m[:, 0], pos_e[:], hot[:, 0], ALU.mult)
            step(v.tensor_tensor(pos_m[:, 1], pos_e[:], hot[:, 1], ALU.mult))
            step(v.tensor_reduce(pos[:], pos_m[:].rearrange("p k t e -> p (k t) e"), axis=AX.X, op=ALU.add))
            step(v.tensor_copy(pos_i[:], pos[:]))
            v.tensor_scalar(blk_i[:], pos_i[:], P.bit_length() - 1, None, ALU.logical_shift_right)
            step(v.tensor_scalar(row_i[:], pos_i[:], P - 1, None, ALU.bitwise_and))
            v.tensor_copy(blk_h[:], blk_i[:])
            step(v.tensor_copy(row_h[:], row_i[:]))
            def over(a, n):
                return a.rearrange("p (o c) -> p o c", o=1).to_broadcast([P, n, a.shape[1]])

            step(v.tensor_tensor(in_block[:], block_no, over(blk_h[:], BLOCKS), ALU.is_equal))
            v.tensor_tensor(marks[:, 0], in_block[:], over(col_no, BLOCKS), ALU.mult)
            v.tensor_scalar(marks[:, 1], in_block[:], lane, None, ALU.mult)
            dve.wait_ge(s["row_no_in"], 16)
            for k in range(K):
                cols = slice(k * TILES, (k + 1) * TILES)
                v.tensor_tensor(in_row[:, :, cols], row_sb[:, :, cols], over(row_h[:, cols], P), ALU.is_equal
                                ).then_inc(s["inrow_done"], 1)
            step(v.scalar_tensor_tensor(end_pos[:], n_blocks[:], float(P), start_pos[:], ALU.mult, ALU.add))
            step(v.tensor_tensor(past[:], end_pos[0:1, :].rearrange("p (o e) -> p o e", o=1)
                                 .to_broadcast([1, BLOCKS, E]), block_at[0:1, :].rearrange("p (b o) -> p b o", o=1)
                                 .to_broadcast([1, BLOCKS, E]), ALU.is_le))
            step(v.tensor_reduce(expert_f[:], past[:], axis=AX.X, op=ALU.add))
            v.tensor_scalar(expert[:], expert_f[:], float(E - 1), None, ALU.min).then_inc(s["expert_done"], 1)
            dve.wait_ge(s["inv_mm"], 1)
            step(v.tensor_scalar(lane_f[:], banks[3][:, BLOCKS:2 * BLOCKS], -1.0, None, ALU.add))
            step(v.scalar_tensor_tensor(pair_f[:], banks[3][:, 0:BLOCKS], float(P), lane_f[:], ALU.mult, ALU.add))
            step(v.tensor_scalar(second[:], pair_f[:], float(T), -float(T), ALU.is_ge, ALU.mult))
            v.scalar_tensor_tensor(src_row[:], pair_f[:], 0.0, second[:], ALU.max, ALU.add).then_inc(s["src_done"], 1)
            step(v.scalar_tensor_tensor(spare[:], pair_f[:], 0.0, spare_row, ALU.is_lt, ALU.mult))
            v.scalar_tensor_tensor(dst_row[:], pair_f[:], 0.0, spare[:], ALU.max, ALU.add).then_inc(s["dst_done"], 1)
            dve.wait_ge(s["ex_done"], 1)
            step(v.tensor_reduce(den[:], dist[:], axis=AX.X, op=ALU.add))
            step(v.reciprocal(c_rec[:], den[:]))
            step(v.tensor_scalar(weight[:, 0], c_rec[:], 0.5, None, ALU.mult))
            v.tensor_tensor(weight[:, 1], weight[:, 0], top2[:], ALU.mult).then_inc(s["weight_done"], 1)

            def silu(b, par):
                dve.wait_ge(s["b_th"], b + 1)
                v.scalar_tensor_tensor(gs[par][:], th[par][:], 1.0, gate[par][:, 0:H], ALU.add, ALU.mult
                                       ).then_inc(s["b_gs"], 1)
                dve.wait_ge(s["b_gs"], b + 1)
                v.tensor_tensor(hid[par][:, 0:H], gs[par][:], val[par][:, 0:H], ALU.mult
                                ).then_inc(s["b_hid"], 1)

            def move_y(b, m):
                dve.wait_ge(s["b_dn"], b + 1)
                dve.wait_ge(s["ys_free"], b + 1)
                v.tensor_copy(ys[m][:], y_bank[:, 0:D]).then_inc(s["b_y"], 1)

            dve.wait_ge(s["zeroed"], 1)
            silu(0, 0)
            silu(1, 1)
            with dve.Fori(2, BLOCKS - RING, RING) as i:
                for j in range(RING):
                    move_y(i + j - 2, j)
                    silu(i + j, j % 2)
            b = BLOCKS - 1
            move_y(b - 2, (b - 2) % RING)
            silu(b, b % 2)
            for c in (b - 1, b):
                move_y(c, c % RING)

            def c_combine(n):
                dve.wait_ge(yb_in[n], 32)
                dve.wait_ge(s["skip"], n + 1)
                if n == 0:
                    dve.wait_ge(s["weight_done"], 1)
                for k, onto in ((0, skip), (1, xg)):
                    if k:
                        dve.wait_ge(s["c_step"], n + 1)
                    for t in range(G):
                        last = v.scalar_tensor_tensor(xg[n][:, t, :], yb[n % 2][:, k, t, :],
                                                      weight[:, k, n * G + t:n * G + t + 1], onto[n][:, t, :],
                                                      ALU.mult, ALU.add)
                    last.then_inc(s["c_x2" if k else "c_step"], 1)

            def c_stats(n):
                dve.wait_ge(s["c_x2"], n + 1)
                stats_of(n, xg, "c_ve")

            def c_shift(n):
                shift_of(n, "c_rstd", "c_shift")

            def c_max(n):
                dve.wait_ge(s["c_sc"], n + 1)
                v.tensor_reduce(nmax[n][:], c_at_bank[:, 0:G * J].rearrange("p (t j) -> p t j", j=J), axis=AX.X,
                                op=ALU.max, negate=True).then_inc(s["c_max"], 1)

            def c_recip(n):
                dve.wait_ge(s["c_exp"], n + 1)
                v.reciprocal(rinv[n][:], rsum[n][:]).then_inc(s["c_rinv"], 1)

            def c_res(n):
                dve.wait_ge(s["c_rinv"], n + 1)
                dve.wait_ge(s["c_pv"], n + 1)
                for t in range(G):
                    last = v.scalar_tensor_tensor(x1[n][:, t, :], c_pv_bank[:, t * D:(t + 1) * D],
                                                  rinv[n][:, t:t + 1], xg[n][:, t, :], ALU.mult, ALU.add)
                last.then_inc(s["c_x3"], 1)

            def c_stats4(n):
                dve.wait_ge(s["c_x3"], n + 1)
                stats_of(n, x1, "c_ve4")

            def c_z(n):
                dve.wait_ge(s["c_rstd4"], n + 1)
                norm(xh, x1, n, rstd[n][:, 0], "c_z")

            def c_mix(n):
                dve.wait_ge(s["c_dz"], n + 1)
                if n >= 2:
                    dve.wait_ge(s["c_k"], n - 1)
                v.scalar_tensor_tensor(xk[n % 2][:], dz[n % 2][:], mu_k_sb, xt[n][:, 0:S], ALU.mult, ALU.add
                                       ).then_inc(s["c_xk"], 1)

            def c_gate(n):
                dve.wait_ge(s["c_tg"], n + 1)
                dve.wait_ge(s["c_kv"], n + 1)
                xh_n = xh[n][:].rearrange("p t d -> p (t d)")
                v.scalar_tensor_tensor(xh_n, xh_n, 1.0, c_kv_bank[:], ALU.add, ALU.mult).then_inc(s["c_wv"], 1)

            for stage, n in staggered(((2.5, c_combine), (5.1, c_stats), (8.2, c_shift), (13.9, c_max),
                                       (19.3, c_recip), (19.4, c_res), (21.3, c_stats4), (23.5, c_z), (27.5, c_mix),
                                       (34.7, c_gate)), LAG1):
                stage(n)


def shape_constants():
    c = np.zeros((P, C_ALL), np.float32)
    p = np.arange(P)
    c[:, C_IDENT:C_FIRST] = np.eye(P)
    c[:, C_FIRST:C_LOWER] = np.tile(E - np.arange(E), TILES)
    c[:, C_LOWER:C_BLOCK] = P * np.tril(np.ones((E, E)), -1).reshape(-1)
    c[:, C_BLOCK:C_SPARE] = np.arange(BLOCKS) * P
    c[:, C_SPARE:C_STEP] = PAIRS + np.arange(BLOCKS) * P + p[:, None]
    c[:, C_STEP:C_LANE] = np.arange(T // P) * P
    c[:, C_LANE] = 1 + p
    m = np.zeros((P, M_ALL), np.float16)
    tile_of, expert_of = np.divmod(np.arange(TILES * E), E)
    m[:, M_BEFORE:M_ONES] = p[:, None] < p
    m[:, M_ONES:M_EARLIER] = 1
    m[:, M_EARLIER:M_SAME] = (expert_of[:, None] == expert_of) & (tile_of[:, None] < tile_of)
    m[:, M_SAME:M_BLOCK] = expert_of[:, None] == np.arange(E)
    m[:, M_BLOCK:M_COL] = np.repeat(np.arange(BLOCKS), COLS)
    m[:, M_COL:M_ALL] = np.arange(COLS)
    rows = np.broadcast_to(np.repeat(p, COLS), (P, P * COLS)).astype(np.float16)
    return c, m, rows


def kernel(**inputs):
    import concourse.bacc as bacc
    from concourse.bass_utils import run_bass_kernel_spmd

    a = {k: np.asarray(v) for k, v in inputs.items()}
    consts, small, row_no = shape_constants()
    mask = a["mask_1xSxS2_bk0"].reshape(G, P, J).transpose(1, 0, 2)
    arrays = {
        "x": a["x"].reshape(T, D),
        "ctx": a["ctx_1024"].transpose(1, 0, 2),
        "attn_mask": mask,
        "row_mask": a["mask_BxS2_if1"].reshape(1, B * J),
        "keys": np.concatenate((a["L0_xattn_wi"], a["L0_xattn_wi"].T, a["ctx_1024"].reshape(B * J, D).T), axis=1),
        "weights": np.concatenate((
            a["L1_xattn_W"].T, a["L1_ffn_W_r"].T, a["L1_ffn_W_k"].T, a["L1_ffn_W_v"].T, a["L0_ffn_w_router"].T,
            a["L0_ffn_norm_scale"].reshape(D, 1), a["L1_xattn_diagonal"].reshape(D, 1),
            a["L1_ffn_mu_r"].reshape(D, 1), a["L1_ffn_mu_k"].reshape(D, 1)), axis=1),
        "up_t": a["L0_ffn_w_up"].transpose(2, 0, 1),
        "down_t": a["L0_ffn_w_down"].transpose(2, 0, 1),
        "consts": consts,
        "small": small,
        "row_no": row_no,
    }
    arrays = {k: np.ascontiguousarray(v) for k, v in arrays.items()}
    nc = bacc.Bacc("TRN2", target_bir_lowering=False, num_devices=1)
    aps = [nc.dram_tensor(f"in_{k}", v.shape, mybir.dt.from_np(v.dtype), kind="ExternalInput").ap()
           for k, v in arrays.items()]
    out = nc.dram_tensor("out_rows", (T, D), F32, kind="ExternalOutput").ap()
    build(nc, *aps, out)
    r = run_bass_kernel_spmd(nc, [{f"in_{k}": v for k, v in arrays.items()}], core_ids=[0])
    return r.results[0]["out_rows"].reshape(B, S, D)
```

```python
from contextlib import ExitStack

import numpy as np
import concourse.bass as bass
from concourse import mybir

F32 = mybir.dt.float32
F32R = mybir.dt.float32r
F16 = mybir.dt.float16
I32 = mybir.dt.int32
U8 = mybir.dt.uint8
ALU = mybir.AluOpType
ACT = mybir.ActivationFunctionType
AX = mybir.AxisListType

P = 128
B, S, D = 4, 512, 128
J = 77
E, H = 8, 352
K = 2
T = B * S
TILES = T // P
G = S // P
PAIRS = K * T
BLOCKS = (PAIRS + E * (P - 1)) // P
HC = (H + P - 1) // P
HP = HC * P
H_LAST = H - (HC - 1) * P
SLOTS = BLOCKS * P
RING = 4
ROWS = 2 * K * G
AHEAD = 10
LAG0, LAG1 = 3.3, 3.0
UNROLL = 16
LOOP_END = 2 + (BLOCKS - 4) // UNROLL * UNROLL
WARM_WAIT, WARM_STAGES, WARM_STAGE = 110, 2, 8
LAG = 2
LN_EPS, RMS_EPS = 1e-5, 1e-6
MASKED = -1e10
FREE = 3.0e38

C_IDENT = 0
C_FIRST = C_IDENT + P
C_LOWER = C_FIRST + TILES * E
C_BLOCK = C_LOWER + E * E
C_SPARE = C_BLOCK + BLOCKS
C_STEP = C_SPARE + BLOCKS
C_LANE = C_STEP + T // P
C_ALL = C_LANE + 1
COLS = K * TILES
PARTS = 4
M_BEFORE = 0
M_ONES = M_BEFORE + P
M_EARLIER = M_ONES + P
M_SAME = M_EARLIER + TILES * E
M_BLOCK = M_SAME + E
M_COL = M_BLOCK + BLOCKS * COLS
M_ALL = M_COL + COLS
A_WI = 0
A_WI_T = A_WI + D
A_CTX_T = A_WI_T + D
A_ALL = A_CTX_T + B * J
W_W1 = 0
W_WR = W_W1 + D
W_WK = W_WR + D
W_WV = W_WK + D
W_ROUTER = W_WV + D
W_SCALE = W_ROUTER + E
W_DIAG = W_SCALE + 1
W_MU_R = W_DIAG + 1
W_MU_K = W_MU_R + 1
W_ALL = W_MU_K + 1


def build(nc, x, ctx, attn_mask, row_mask, keys, weights, up_t, down_t, consts, small, row_no, out):
    with ExitStack() as stack:
        def sb(name, shape, dt=F32):
            return stack.enter_context(nc.sbuf_tensor(name, shape, dt))

        def each(name, shape, dt=F32, n=B):
            return [sb(f"{name}{g}", shape, dt) for g in range(n)]

        def sem(name):
            return stack.enter_context(nc.semaphore(name))

        xn_dram = nc.dram_tensor("xn_rows", [T, D], F32).ap()
        y_dram = nc.dram_tensor("y_rows", [P + PAIRS + SLOTS, D], F32).ap()

        banks = [stack.enter_context(nc.psum_tensor(f"bank{n}", [P, 512], F32)) for n in range(8)]

        cst = sb("cst", [P, C_ALL])
        m16 = sb("m16", [P, M_ALL], F16)
        row_sb = sb("row_sb", [P, P, COLS], F16)
        ident = cst[:, C_IDENT:C_FIRST]
        first_w = cst[:, C_FIRST:C_LOWER].rearrange("p (t e) -> p t e", e=E)
        lower = cst[:, C_LOWER:C_BLOCK].rearrange("p (e f) -> p e f", f=E)
        block_at = cst[:, C_BLOCK:C_SPARE]
        spare_row = cst[:, C_SPARE:C_STEP]
        step_no = cst[:, C_STEP:C_LANE]
        lane = cst[:, C_LANE:C_ALL]
        block_no = m16[:, M_BLOCK:M_COL].rearrange("p (b c) -> p b c", c=COLS)
        col_no = m16[:, M_COL:M_ALL]
        ctx_sb = sb("ctx_sb", [J, B, D])
        mask_sb = sb("mask_sb", [P, G, J], U8)
        row_mask_sb = sb("row_mask_sb", [1, B * J], I32)
        keys_sb = sb("keys_sb", [P, A_ALL])
        wi_sb, wi_t_sb, ctx_t_sb = (keys_sb[:, a:b] for a, b in (
            (A_WI, A_WI_T), (A_WI_T, A_CTX_T), (A_CTX_T, A_ALL)))
        weights_sb = sb("weights_sb", [P, W_ALL])
        w1_sb, wr_sb, wk_sb, wv_sb, router_sb, scale_sb, diag_sb, mu_r_sb, mu_k_sb = (
            weights_sb[:, a:b] for a, b in (
                (W_W1, W_WR), (W_WR, W_WK), (W_WK, W_WV), (W_WV, W_ROUTER), (W_ROUTER, W_SCALE),
                (W_SCALE, W_DIAG), (W_DIAG, W_MU_R), (W_MU_R, W_MU_K), (W_MU_K, W_ALL)))
        up_sb = sb("up_sb", [P, E, 2 * H])
        up_hi = sb("up_hi", [P, E, 2 * H], F32R)
        up_lo = up_sb[:].bitcast(F32R)
        down_sb = sb("down_sb", [P, HC, E, D])
        ones_g = sb("ones_g", [P, G])
        power = sb("power", [P, G])

        kt0 = sb("kt0", [P, B * J])
        qs_rhs = sb("qs_rhs", [P, B, D + J])
        v0 = sb("v0", [J, B, D])
        cap = sb("cap", [P, G, J])
        router_s = sb("router_s", [P, E])
        k1 = sb("k1", [P, B, J])
        add1 = sb("add1", [1, B, G, J])
        add1_b = sb("add1_b", [1, B * J])
        ones_row = sb("ones_row", [1, P])
        one_mu = sb("one_mu", [P, 1])
        wr_now = sb("wr_now", [P, D])
        wr_prev = sb("wr_prev", [P, D])
        wv_half = sb("wv_half", [P, D])

        xg = each("xg", [P, G, D])
        stats = each("stats", [P, G, 6])
        mv = each("mv", [P, G, 2])
        shift = each("shift", [P, G])
        ve = each("ve", [P, 2, G])
        rstd = each("rstd", [P, 2, G])
        gain = each("gain", [P, G])
        offset = each("offset", [P, G])
        xh = each("xh", [P, G, D])
        xt = each("xt", [P, S + 1])
        sm = each("sm", [P, G, J])
        nmax = each("nmax", [P, G])
        pr = each("pr", [P, G, J])
        rsum = each("rsum", [P, G])
        rinv = each("rinv", [P, G])
        pt = each("pt", [J, S])
        x1 = each("x1", [P, G, D])
        xn = each("xn", [P, G, D])
        skip = each("skip", [P, G, D])
        yb = each("yb", [P, K, G, D], n=2)
        xk = each("xk", [P, S], n=2)
        rk = each("rk", [P, S], n=2)
        dz = each("dz", [P, S], n=2)

        def route(name, shape=(P, TILES, E), dt=F32):
            return sb(name, list(shape), dt)

        sc, eq, sc2, dist = (route(n) for n in ("sc", "eq", "sc2", "dist"))
        top1, top2, pick1, pick2, den, c_rec = (route(n, (P, TILES)) for n in (
            "top1", "top2", "pick1", "pick2", "den", "c_rec"))
        weight = route("weight", (P, K, TILES))
        hot = sb("hot", [P, K, TILES, E])
        hot16 = route("hot16", dt=F16)
        counts = sb("counts", [P, P], F16)
        n_gt = sb("n_gt", [P, E, T // P])
        n_blocks = sb("n_blocks", [P, E])
        tri = sb("tri", [P, E, E])
        start_pos = sb("start_pos", [P, E])
        end_pos = sb("end_pos", [P, E])
        pos_e = route("pos_e")
        pos_m = sb("pos_m", [P, K, TILES, E])
        pos = sb("pos", [P, COLS])
        pos_i = sb("pos_i", [P, COLS], I32)
        blk_i = sb("blk_i", [P, COLS], I32)
        row_i = sb("row_i", [P, COLS], I32)
        blk_h = sb("blk_h", [P, COLS], F16)
        row_h = sb("row_h", [P, COLS], F16)
        in_block = sb("in_block", [P, BLOCKS, COLS], F16)
        marks = sb("marks", [P, 2, BLOCKS, COLS], F16)
        past = sb("past", [1, BLOCKS, E])
        expert_f = sb("expert_f", [1, BLOCKS])
        expert = sb("expert", [1, BLOCKS + UNROLL], I32)
        pair_f = sb("pair_f", [P, BLOCKS])
        pair_i = sb("pair_i", [P, BLOCKS], I32)
        spare = sb("spare", [P, BLOCKS])
        src_row = sb("src_row", [P, BLOCKS], I32)
        dst_row = sb("dst_row", [P, BLOCKS], I32)

        rows = [buf[:, k, g, :] for buf in yb for k in range(K) for g in range(G)]
        rows_hi = each("rows_hi", [P, P], F32R, n=2)
        rows_lo = each("rows_lo", [P, P], F32R, n=2)
        th, gs, hid = ([buf[:, 0:w] for buf in bufs] for bufs, w in ((xk, H), (rk, H), (dz, HP)))
        hid_t = each("hid_t", [P, HP], n=2)
        ys = each("ys", [P, D], n=RING)

        NAMES = """keys_in weights_in ctx_in consts_in small_in row_no_in mask_in down_in zeroed
            kt0_mm kt0_sb qs_mm v0_mm k1_mm wi_copied cap_done setup_dve setup_act setup_step
            st ve rstd shift xh xt_mm xt qs sm max exp rinv pr pt_mm pt pv x1 ve2 rstd_x rstd_y
            shift2 xn xn_mm xnt rt sc_sb pool_step skip
            step hot_done prefix_mm counts_done totals_mm dist_done ex_done row_done block_done marks0_done marks1_done inrow_done
            up_hi_done up_lo_done inv_mm src_done dst_done expert_done weight_done
            b_xt_mm b_xt b_lo b_up b_th b_gs b_hid b_ht_mm b_ht b_dn b_y ys_free
            c_step c_x2 c_ve c_rstd c_shift c_xh c_xt_mm c_xt c_rt_mm c_rt c_sc c_max c_exp c_rinv
            c_pt_mm c_pt c_pv c_x3 c_ve4 c_rstd4 c_z c_zt_mm c_zt c_dz c_xk c_k c_r c_rk c_ka
            c_tg c_kv c_wv c_res c_last""".split()
        s = {n: sem(n) for n in NAMES}
        x_in = [sem(f"x_in{n}") for n in range(B)]
        up_in = [sem(f"up_in{n}") for n in range(B)]
        xn_out = sem("xn_out")
        rows_in = [sem(f"rows_in{m}") for m in range(ROWS)]
        ys_out = [sem(f"ys_out{m}") for m in range(RING)]
        yb_in = [[sem(f"yb_in{n}_{k}") for k in range(K)] for n in range(B)]
        res_out = sem("res_out")

        def scores0(n, half):
            return banks[2 * (n % 2) + half][:, 0:2 * (D + J)].rearrange("p (t c) -> p t c", t=2)

        xh_bank, pr_bank, xn_bank, route_bank = banks[4], banks[5], banks[6], banks[7]
        gate, val = [banks[0], banks[1]], [banks[2], banks[3]]
        rt_bank, ht_bank = [banks[4], banks[7]], [banks[5], banks[6]]
        c_xh_bank, c_rt_bank, c_at_bank, c_pv_bank, c_z_bank, c_k_bank, c_r_bank, c_kv_bank = banks

        def over(a, n):
            return a.rearrange("p (o c) -> p o c", o=1).to_broadcast([P, n, a.shape[1]])

        def tiles_in(dram, n):
            return dram[n * S:(n + 1) * S, :].rearrange("(t p) d -> p t d", p=P)

        def all_scattered(program):
            for m in range(RING):
                program.wait_ge(ys_out[m], 16 * ((BLOCKS - m + RING - 1) // RING))

        def load_y(program, n, k):
            program.dma_start(yb[n % 2][:, k], tiles_in(y_dram[P + k * T:P + (k + 1) * T, :], n)
                              ).then_inc(yb_in[n][k], 16)

        def staggered(stages, lag):
            return [(f, n) for _, n, f in sorted(
                ((at + lag * n, n, f) for at, f in stages for n in range(B)), key=lambda x: x[:2])]

        block = stack.enter_context(nc.Block())

        @block.sync
        def _(sp):
            sp.dma_start(keys_sb[:], keys).then_inc(s["keys_in"], 16)
            sp.dma_start(xg[0][:], tiles_in(x, 0)).then_inc(x_in[0], 16)
            sp.dma_start(mask_sb[:], attn_mask).then_inc(s["mask_in"], 16)
            sp.dma_start(weights_sb[:], weights).then_inc(s["weights_in"], 16)
            sp.dma_start(xg[1][:], tiles_in(x, 1)).then_inc(x_in[1], 16)
            sp.dma_start(row_mask_sb[:], row_mask).then_inc(s["mask_in"], 16)
            sp.dma_start(cst[:], consts).then_inc(s["consts_in"], 16)
            for n in range(2, B):
                sp.dma_start(xg[n][:], tiles_in(x, n)).then_inc(x_in[n], 16)
            sp.dma_start(m16[:], small).then_inc(s["small_in"], 16)
            sp.dma_start(row_sb[:].rearrange("p r c -> p (r c)"), row_no).then_inc(s["row_no_in"], 16)
            sp.dma_start(ctx_sb[:], ctx).then_inc(s["ctx_in"], 16)
            for n in range(B):
                part = slice(n * E // B, (n + 1) * E // B)
                sp.dma_start(up_sb[:, part], up_t[:, part]).then_inc(up_in[n], 16)
            sp.dma_start(down_sb[:, 0:HC - 1], down_t[0:(HC - 1) * P].rearrange("(c p) e d -> p c e d", p=P)
                         ).then_inc(s["down_in"], 16)
            sp.dma_start(down_sb[0:H_LAST, HC - 1], down_t[(HC - 1) * P:H]).then_inc(s["down_in"], 16)
            for n in range(B):
                sp.wait_ge(s["xn"], (n + 1) * G)
                first = n * G + 1
                ahead = min(G, TILES - first)
                sp.dma_start(xn_dram[first * P:(first + ahead) * P, :].rearrange("(t p) d -> p t d", p=P),
                             xn[n][:, 0:ahead]).then_inc(xn_out, 16)
                if ahead < G:
                    sp.dma_start(xn_dram[0:P, :], xn[n][:, ahead]).then_inc(xn_out, 16)
            all_scattered(sp)
            for n in range(B):
                if n >= 2:
                    sp.wait_ge(s["c_x2"], n - 1)
                for k in range(K):
                    if (n, k) != (0, K - 1):
                        load_y(sp, n, k)
            for n in range(B):
                if n < B - 1:
                    sp.wait_ge(s["c_res"], n + 1)
                else:
                    sp.wait_ge(s["c_last"], 1)
                sp.dma_start(tiles_in(out, n), xh[n][:]).then_inc(res_out, 16)
            sp.wait_ge(res_out, 16 * B)
            sp.wait_ge(xn_out, 16 * (B + 1))

        @block.gpsimd
        def _(pool):
            nc.gpsimd.memset(power[:], -0.5)
            nc.gpsimd.memset(ones_g[:], 1.0)
            for m in range(2):
                nc.gpsimd.memset(hid[m][:, H:HP], 0.0)
            for n in range(B):
                nc.gpsimd.memset(xt[n][:, 0:1], 0.0)
            nc.gpsimd.memset(ones_row[:], 1.0).then_inc(s["zeroed"], 1)
            pool.wait_ge(s["zeroed"], 1)
            pool.sem_inc(s["ys_free"], RING)

            def root(n, row, ready, signal):
                pool.wait_ge(s[ready], n + 1)
                nc.gpsimd.tensor_tensor(rstd[n][:, row], ve[n][:, row], power[:], ALU.pow
                                        ).then_inc(s[signal], 1)

            def rstd0(n):
                root(n, 0, "ve", "rstd")

            def rstd_xn(n):
                root(n, 1, "ve2", "rstd_x")

            def rstd_y(n):
                root(n, 0, "ve2", "rstd_y")

            def skip0(n):
                pool.wait_ge(s["rstd_y"], n + 1)
                nc.gpsimd.tensor_tensor(gain[n][:], rstd[n][:, 0], ones_g[:], ALU.add)
                nc.gpsimd.tensor_tensor(offset[n][:], mv[n][:, :, 0], rstd[n][:, 0], ALU.mult
                                        ).then_inc(s["pool_step"], 1)
                pool.wait_ge(s["pool_step"], 2 * n + 1)
                nc.gpsimd.tensor_tensor(skip[n][:], x1[n][:], gain[n][:].rearrange("p (t o) -> p t o", o=1)
                                        .to_broadcast([P, G, D]), ALU.mult).then_inc(s["pool_step"], 1)
                pool.wait_ge(s["pool_step"], 2 * n + 2)
                nc.gpsimd.tensor_tensor(skip[n][:], skip[n][:], offset[n][:].rearrange("p (t o) -> p t o", o=1)
                                        .to_broadcast([P, G, D]), ALU.subtract).then_inc(s["skip"], 1)

            for stage, n in staggered(((4, rstd0), (18.8, rstd_xn), (20.2, rstd_y), (22.2, skip0)), LAG0):
                stage(n)

            for e in range(E):
                pool.wait_ge(s["up_hi_done"], e + 1)
                nc.gpsimd.tensor_tensor(up_lo[:, e], up_sb[:, e], up_hi[:, e].bitcast(F32), ALU.subtract
                                        ).then_inc(s["up_lo_done"], 1)

            def gather(b):
                if b >= ROWS:
                    pool.wait_ge(s["b_xt_mm"], b - ROWS + 1)
                pool.indirect_dma_start(
                    out=rows[b % ROWS], out_offset=None, in_=xn_dram,
                    in_offset=bass.IndirectOffsetOnAxis(ap=src_row[:, b:b + 1], axis=0),
                ).then_inc(rows_in[b % ROWS], 16)

            def scatter(b):
                if b >= LAG:
                    pool.wait_ge(ys_out[(b - LAG) % RING], 16 * ((b - LAG) // RING + 1))
                    pool.sem_inc(s["ys_free"], 1)
                pool.wait_ge(s["b_y"], b + 1)
                pool.indirect_dma_start(
                    out=y_dram, out_offset=bass.IndirectOffsetOnAxis(ap=dst_row[:, b:b + 1], axis=0),
                    in_=ys[b % RING][:], in_offset=None,
                ).then_inc(ys_out[b % RING], 16)

            pool.wait_ge(xn_out, 16 * (B + 1))
            pool.wait_ge(s["src_done"], 1)
            for b in range(AHEAD):
                gather(b)
            pool.wait_ge(s["dst_done"], 1)
            for b in range(BLOCKS):
                if b + AHEAD < BLOCKS:
                    gather(b + AHEAD)
                scatter(b)

            def rstd3(n):
                root(n, 0, "c_ve", "c_rstd")

            def rstd4(n):
                root(n, 0, "c_ve4", "c_rstd4")

            def before(n):
                pool.wait_ge(s["c_zt"], n + 1)
                if n >= 2:
                    pool.wait_ge(s["c_xk"], n - 1)
                nc.gpsimd.tensor_tensor(dz[n % 2][:], xt[n][:, 1:S + 1], xt[n][:, 0:S], ALU.subtract
                                        ).then_inc(s["c_dz"], 1)

            def add_mix(n):
                if n == B - 1:
                    return
                pool.wait_ge(s["c_wv"], n + 1)
                nc.gpsimd.tensor_tensor(xh[n][:], xh[n][:], x1[n][:], ALU.add).then_inc(s["c_res"], 1)

            for stage, n in staggered(((2, rstd3), (20.2, rstd4), (21, before), (32.8, add_mix)), LAG1):
                stage(n)

        @block.tensor
        def _(pe):
            mm = nc.tensor.matmul
            def keep_warm(count, bank):
                for _ in range(count):
                    mm(bank[:, 0:2 * P], m16[:, 0:P], m16[:, 0:2 * P], start=True, stop=True)

            pe.wait_ge(s["keys_in"], 16)
            mm(banks[0][:, 0:B * J], wi_sb, ctx_t_sb, start=True, stop=True).then_inc(s["kt0_mm"], 1)
            for b in range(B):
                last = mm(banks[1][0:J, b * D:(b + 1) * D], ctx_t_sb[:, b * J:(b + 1) * J], wi_sb,
                          start=True, stop=True)
            last.then_inc(s["v0_mm"], 1)
            pe.wait_ge(s["kt0_sb"], 1)
            mm(banks[2][:, 0:B * J], wi_t_sb, kt0[:], start=True, stop=True).then_inc(s["qs_mm"], 1)
            pe.wait_ge(s["weights_in"], 16)
            mm(pr_bank[:, 0:B * J], w1_sb, ctx_t_sb, start=True, stop=True).then_inc(s["k1_mm"], 1)
            pe.wait_ge(s["consts_in"], 16)

            def transpose_group(n, bank, src, ready, signal, rows_out=P, by_tile=True):
                if not by_tile:
                    pe.wait_ge(s[ready], n + 1)
                for t in range(G):
                    if by_tile:
                        pe.wait_ge(s[ready], n * G + t + 1)
                    last = nc.tensor.transpose(bank[0:rows_out, t * P:(t + 1) * P], src[n][:, t, :], ident)
                last.then_inc(s[signal], 1)

            def tile_t(buf, n, t, back=0):
                return buf[n][:, 1 + t * P - back:1 + (t + 1) * P - back]

            def t_xh(n):
                if n:
                    pe.wait_ge(s["xt"], n)
                transpose_group(n, xh_bank, xh, "xh", "xt_mm")

            def qs(n):
                pe.wait_ge(s["xt"], n + 1)
                if n == 0:
                    pe.wait_ge(s["setup_act"], 1)
                    pe.wait_ge(s["wi_copied"], 1)
                if n >= 2:
                    pe.wait_ge(s["x1"], n - 1)
                for t in range(G):
                    last = mm(scores0(n, t // 2)[:, t % 2, :], tile_t(xt, n, t), qs_rhs[:, n, :],
                              start=(t % 2 == 0), stop=(t % 2 == 1), skip_group_check=True)
                last.then_inc(s["qs"], 1)

            def t_pr(n):
                if n:
                    pe.wait_ge(s["pt"], n)
                else:
                    pe.wait_ge(s["setup_dve"], 1)
                transpose_group(n, pr_bank, pr, "pr", "pt_mm", J, by_tile=False)

            def pv(n):
                pe.wait_ge(s["pt"], n + 1)
                for t in range(G):
                    last = mm(scores0(n, t // 2)[:, t % 2, 0:D], pt[n][:, t * P:(t + 1) * P], v0[:, n, :],
                              start=False, stop=True, skip_group_check=True)
                last.then_inc(s["pv"], 1)

            def t_xn(n):
                if n:
                    pe.wait_ge(s["xnt"], n)
                transpose_group(n, xn_bank, xn, "xn", "xn_mm")

            def router(n):
                pe.wait_ge(s["xnt"], n + 1)
                if n:
                    pe.wait_ge(s["sc_sb"], n)
                for t in range(G):
                    last = mm(route_bank[:, t * E:(t + 1) * E], tile_t(xt, n, t), router_s[:],
                              start=True, stop=True)
                last.then_inc(s["rt"], 1)

            for stage, n in staggered(((8.3, t_xh), (9.7, qs), (13.4, t_pr), (15.5, pv), (21.9, t_xn),
                                       (23.2, router)), LAG0):
                stage(n)

            prefix = banks[0][:, 0:TILES * E]
            pe.wait_ge(s["small_in"], 16)
            pe.wait_ge(s["hot_done"], B)
            hot2d = hot16[:].rearrange("p t e -> p (t e)")
            mm(banks[1][:, 0:P], hot2d, m16[:, M_ONES:M_ONES + P], start=True, stop=True).then_inc(s["prefix_mm"], 1)
            mm(prefix, m16[:, M_BEFORE:M_BEFORE + P], hot2d, start=True, stop=False)
            pe.wait_ge(s["counts_done"], 1)
            mm(banks[2][:, 0:E], counts[:], m16[:, M_SAME:M_SAME + E], start=True, stop=True)
            mm(prefix, counts[:], m16[:, M_EARLIER:M_EARLIER + TILES * E], start=False, stop=True
               ).then_inc(s["totals_mm"], 1)
            pe.wait_ge(s["marks0_done"], 1)
            pe.wait_ge(s["marks1_done"], 1)
            for c in range(COLS):
                if c % (COLS // PARTS) == 0:
                    pe.wait_ge(s["inrow_done"], c // (COLS // PARTS) + 1)
                last = mm(banks[3][:, 0:2 * BLOCKS], row_sb[:, :, c], marks[:, :, :, c],
                          start=(c == 0), stop=(c == COLS - 1))
            last.then_inc(s["inv_mm"], 1)

            def t_rows(b, m, par, landed):
                pe.wait_ge(rows_in[m], landed)
                nc.tensor.transpose(rt_bank[par][:, 0:P], rows[m], ident).then_inc(s["b_xt_mm"], 1)

            def expert_of(b):
                return pe.value_load(expert[0:1, bass.ds(b, 1)], min_val=0, max_val=E - 1)

            def up(b, par, e):
                pe.wait_ge(s["b_lo"], b + 1)
                for dst, at in ((gate[par], H), (val[par], 0)):
                    w_hi, w_lo = (w[:, bass.ds(e, 1), at:at + H].rearrange("p o c -> p (o c)")
                                  for w in (up_hi, up_lo))
                    mm(dst[:, 0:H], rows_hi[par][:], w_hi, start=True, stop=False)
                    mm(dst[:, 0:H], rows_hi[par][:], w_lo, start=False, stop=False)
                    last = mm(dst[:, 0:H], rows_lo[par][:], w_hi, start=False, stop=True)
                last.then_inc(s["b_up"], 1)

            def t_hid(b, par):
                pe.wait_ge(s["b_hid"], b + 1)
                for c in range(HC):
                    last = nc.tensor.transpose(ht_bank[par][:, c * P:(c + 1) * P],
                                               hid[par][:, c * P:(c + 1) * P], ident)
                last.then_inc(s["b_ht_mm"], 1)

            def down(b, par, e):
                pe.wait_ge(s["b_ht"], b + 1)
                for c in range(HC):
                    kk = P if c < HC - 1 else H_LAST
                    last = mm(ht_bank[par][:, HP:HP + D], hid_t[par][0:kk, c * P:(c + 1) * P],
                              down_sb[0:kk, c, bass.ds(e, 1), :].rearrange("p o c -> p (o c)"),
                              start=(c == 0), stop=(c == HC - 1))
                last.then_inc(s["b_dn"], 1)

            pe.wait_ge(s["expert_done"], 1)
            pe.wait_ge(s["dst_done"], 1)
            pe.wait_ge(s["down_in"], 32)
            pe.wait_ge(s["up_lo_done"], E)
            first, second = expert_of(0), expert_of(1)
            t_rows(0, 0, 0, 16)
            t_rows(1, 1, 1, 16)
            up(0, 0, first)
            t_rows(2, 2, 0, 16)
            up(1, 1, second)
            t_rows(3, 3, 1, 16)
            t_hid(0, 0)
            def step(first, j, count, place, landed):
                b, par = first + j, j % 2
                if j == 0:
                    e_of[0] = expert_of(b)
                up(b, par, e_of[j])
                if place is not None:
                    t_rows(b + 2, place, par, landed)
                if j + 1 < count:
                    e_of[j + 1] = expert_of(b + 1)
                down(b - 2, par, e_of[j - 2] if j >= 2 else expert_of(b - 2))
                t_hid(b - 1, 1 - par)

            with pe.Fori(2, LOOP_END, UNROLL) as i:
                e_of = {}
                for j in range(UNROLL):
                    turn, place = divmod(j + 4, ROWS)
                    step(i, j, UNROLL, place, i + (16 * (turn + 1) - 2))
            e_of = {}
            for b in range(LOOP_END, BLOCKS):
                place = (b + 2) % ROWS if b + 2 < BLOCKS else None
                step(LOOP_END, b - LOOP_END, BLOCKS - LOOP_END, place, 16 * ((b + 2) // ROWS + 1))
            down(b - 1, (b - 1) % 2, e_of[b - 1 - LOOP_END])
            t_hid(b, b % 2)
            down(b, b % 2, e_of[b - LOOP_END])

            keep_warm(WARM_WAIT, c_kv_bank)

            def c_t_xh(n):
                if n:
                    pe.wait_ge(s["c_xt"], n)
                transpose_group(n, c_xh_bank, xh, "c_xh", "c_xt_mm")

            def c_rt(n):
                pe.wait_ge(s["c_xt"], n + 1)
                if n:
                    pe.wait_ge(s["c_rt"], n)
                mm(c_rt_bank[:], w1_sb, xt[n][:, 1:S + 1], start=True, stop=True).then_inc(s["c_rt_mm"], 1)

            def c_scores(n):
                pe.wait_ge(s["c_rt"], n + 1)
                if n:
                    pe.wait_ge(s["c_pt"], n)
                mm(c_at_bank[:, 0:G * J], ones_row[:], add1[:, n, :, :].rearrange("p t j -> p (t j)"),
                   start=True, stop=False, skip_group_check=True)
                for t in range(G):
                    last = mm(c_at_bank[:, t * J:(t + 1) * J], xn[n][:, t, :], k1[:, n, :],
                              start=False, stop=(t == G - 1), skip_group_check=True)
                last.then_inc(s["c_sc"], 1)

            def c_t_pr(n):
                transpose_group(n, c_at_bank, pr, "c_exp", "c_pt_mm", J, by_tile=False)

            def c_pv(n):
                pe.wait_ge(s["c_pt"], n + 1)
                if n == 0:
                    pe.wait_ge(s["ctx_in"], 16)
                if n:
                    pe.wait_ge(s["c_x3"], n)
                for t in range(G):
                    last = mm(c_pv_bank[:, t * D:(t + 1) * D], pt[n][:, t * P:(t + 1) * P], ctx_sb[:, n, :],
                              start=True, stop=True)
                last.then_inc(s["c_pv"], 1)

            def c_t_z(n):
                if n:
                    pe.wait_ge(s["c_zt"], n)
                transpose_group(n, c_z_bank, xh, "c_z", "c_zt_mm")

            def c_r(n):
                pe.wait_ge(s["c_zt"], n + 1)
                if n:
                    pe.wait_ge(s["c_tg"], n)
                for t in range(G):
                    mm(c_r_bank[:, t * D:(t + 1) * D], tile_t(xt, n, t), wr_now[:], start=True, stop=False)
                    last = mm(c_r_bank[:, t * D:(t + 1) * D], tile_t(xt, n, t, 1), wr_prev[:],
                              start=False, stop=True)
                last.then_inc(s["c_r"], 1)

            def c_k(n):
                pe.wait_ge(s["c_xk"], n + 1)
                if n:
                    pe.wait_ge(s["c_rk"], n)
                mm(c_k_bank[:], wk_sb, xk[n % 2][:], start=True, stop=True).then_inc(s["c_k"], 1)

            def c_kv(n):
                pe.wait_ge(s["c_ka"], n + 1)
                if n:
                    pe.wait_ge(s["c_wv"], n)
                for t in range(G):
                    last = mm(c_kv_bank[:, t * D:(t + 1) * D], rk[n % 2][:, t * P:(t + 1) * P], wv_half[:],
                              start=True, stop=True)
                last.then_inc(s["c_kv"], 1)

            for place, (stage, n) in enumerate(staggered(((8.8, c_t_xh), (10.4, c_rt), (11.5, c_scores), (13.5, c_t_pr), (15.5, c_pv),
                                       (20.4, c_t_z), (21.5, c_r), (24.1, c_k), (26.3, c_kv)), LAG1)):
                stage(n)
                if place < WARM_STAGES:
                    keep_warm(WARM_STAGE, c_kv_bank)

        @block.scalar
        def _(act):
            act.wait_ge(s["kt0_mm"], 1)
            nc.scalar.activation(kt0[:], banks[0][:, 0:B * J], ACT.Copy).then_inc(s["kt0_sb"], 1)
            act.wait_ge(s["v0_mm"], 1)
            nc.scalar.activation(v0[:], banks[1][0:J, :].rearrange("p (b d) -> p b d", d=D), ACT.Copy)
            act.wait_ge(s["qs_mm"], 1)
            nc.scalar.activation(qs_rhs[:, :, D:D + J], banks[2][:, 0:B * J].rearrange("p (b j) -> p b j", j=J),
                                 ACT.Copy, scale=float(D) ** -0.5).then_inc(s["setup_act"], 1)
            act.wait_ge(s["zeroed"], 1)

            def move_t(n, bank, ready, signal):
                act.wait_ge(s[ready], n + 1)
                nc.scalar.activation(xt[n][:, 1:S + 1], bank[:], ACT.Copy).then_inc(s[signal], 1)

            def move_pt(n, bank, ready, signal):
                act.wait_ge(s[ready], n + 1)
                nc.scalar.activation(pt[n][:], bank[0:J, :], ACT.Copy).then_inc(s[signal], 1)

            def exps(n, src, ready, signal):
                act.wait_ge(s[ready], n + 1)
                for t in range(G):
                    last = nc.scalar.activation(pr[n][:, t, :], src(t), ACT.Exp, bias=nmax[n][:, t:t + 1],
                                                accum_out=rsum[n][:, t:t + 1])
                last.then_inc(s[signal], 1)

            def norm(n, dst, src, ready, signal, row=0):
                act.wait_ge(s[ready], n + 1)
                for t in range(G):
                    nc.scalar.activation(dst[n][:, t, :], src[n][:, t, :], ACT.Identity, bias=shift[n][:, t:t + 1],
                                         scale=rstd[n][:, row, t:t + 1]).then_inc(s[signal], 1)

            def a_norm(n):
                norm(n, xh, xg, "shift", "xh")

            def a_move_xt(n):
                move_t(n, xh_bank, "xt_mm", "xt")

            def a_exp(n):
                exps(n, lambda t: sm[n][:, t, :], "max", "exp")

            def a_move_pt(n):
                move_pt(n, pr_bank, "pt_mm", "pt")

            def a_xn(n):
                norm(n, xn, x1, "shift2", "xn", 1)

            def a_move_xn(n):
                move_t(n, xn_bank, "xn_mm", "xnt")

            for stage, n in staggered(((6.8, a_norm), (8.1, a_move_xt), (11.8, a_exp), (13.9, a_move_pt),
                                       (18.8, a_xn), (21.5, a_move_xn)), LAG0):
                stage(n)

            for e in range(E):
                if e % (E // B) == 0:
                    act.wait_ge(up_in[e // (E // B)], 16)
                nc.scalar.activation(up_hi[:, e], up_sb[:, e], ACT.Copy).then_inc(s["up_hi_done"], 1)

            act.wait_ge(s["dist_done"], B)
            nc.scalar.activation(dist[:], dist[:], ACT.Exp)
            nc.scalar.activation(top2[:], top2[:], ACT.Exp).then_inc(s["ex_done"], 1)
            act.wait_ge(s["block_done"], 1)
            nc.scalar.activation(marks[:, 1], in_block[:], ACT.Copy, scale=lane).then_inc(s["marks1_done"], 1)

            def move_rows(b, par):
                act.wait_ge(s["b_xt_mm"], b + 1)
                nc.scalar.activation(rows_hi[par][:], rt_bank[par][:, 0:P], ACT.Copy, scale=scale_sb
                                     ).then_inc(s["b_xt"], 1)

            def tanh_gate(b, par):
                act.wait_ge(s["b_up"], b + 1)
                nc.scalar.activation(th[par][:], gate[par][:, 0:H], ACT.Tanh, scale=0.5).then_inc(s["b_th"], 1)

            def move_hid(b, par):
                act.wait_ge(s["b_ht_mm"], b + 1)
                nc.scalar.activation(hid_t[par][:], ht_bank[par][:, 0:HP], ACT.Copy).then_inc(s["b_ht"], 1)

            move_rows(0, 0)
            move_rows(1, 1)
            tanh_gate(0, 0)
            move_rows(2, 0)
            tanh_gate(1, 1)
            move_rows(3, 1)
            move_hid(0, 0)
            with act.Fori(2, LOOP_END, UNROLL) as i:
                for j in range(UNROLL):
                    b, par = i + j, j % 2
                    tanh_gate(b, par)
                    move_rows(b + 2, par)
                    move_hid(b - 1, 1 - par)
            for b in range(LOOP_END, BLOCKS):
                tanh_gate(b, b % 2)
                if b + 2 < BLOCKS:
                    move_rows(b + 2, b % 2)
                move_hid(b - 1, (b - 1) % 2)
            move_hid(b, b % 2)

            all_scattered(act)
            load_y(act, 0, K - 1)

            def c_norm(n):
                norm(n, xh, xg, "c_shift", "c_xh")

            def c_move_xt(n):
                move_t(n, c_xh_bank, "c_xt_mm", "c_xt")

            def c_relu_rt(n):
                act.wait_ge(s["c_rt_mm"], n + 1)
                nc.scalar.activation(xn[n][:].rearrange("p t d -> p (t d)"), c_rt_bank[:], ACT.Relu
                                     ).then_inc(s["c_rt"], 1)

            def c_exp(n):
                exps(n, lambda t: c_at_bank[:, t * J:(t + 1) * J], "c_max", "c_exp")

            def c_move_pt(n):
                move_pt(n, c_at_bank, "c_pt_mm", "c_pt")

            def c_move_zt(n):
                move_t(n, c_z_bank, "c_zt_mm", "c_zt")

            def c_relu_k(n):
                act.wait_ge(s["c_k"], n + 1)
                if n >= 2:
                    act.wait_ge(s["c_kv"], n - 1)
                nc.scalar.activation(rk[n % 2][:], c_k_bank[:], ACT.Relu).then_inc(s["c_rk"], 1)
                act.wait_ge(s["c_rk"], n + 1)
                nc.scalar.activation(rk[n % 2][:], rk[n % 2][:], ACT.Square).then_inc(s["c_ka"], 1)

            def c_tanh(n):
                act.wait_ge(s["c_r"], n + 1)
                nc.scalar.activation(xh[n][:].rearrange("p t d -> p (t d)"), c_r_bank[:], ACT.Tanh, scale=0.5
                                     ).then_inc(s["c_tg"], 1)

            for stage, n in staggered(((7.2, c_norm), (8.1, c_move_xt), (9.7, c_relu_rt), (12.1, c_exp),
                                       (13.2, c_move_pt), (20.0, c_move_zt), (21.5, c_tanh), (23.8, c_relu_k)),
                                      LAG1):
                stage(n)

        @block.vector
        def _(dve):
            v = nc.vector
            dve.wait_ge(s["keys_in"], 16)
            for b in range(B):
                last = v.tensor_copy(qs_rhs[:, b, 0:D], wi_sb)
            last.then_inc(s["wi_copied"], 1)

            def setup_rest():
                dve.wait_ge(s["mask_in"], 32)
                v.tensor_scalar(cap[:], mask_sb[:], FREE, MASKED, ALU.mult, ALU.add).then_inc(s["cap_done"], 1)
                dve.wait_ge(s["weights_in"], 16)
                v.tensor_scalar(router_s[:], router_sb, scale_sb, None, ALU.mult)
                v.tensor_scalar(add1_b[:], row_mask_sb[:], 1e4, -1e4, ALU.mult, ALU.add)
                v.tensor_scalar(one_mu[:], mu_r_sb, -1.0, 1.0, ALU.mult, ALU.add).then_inc(s["setup_step"], 1)
                dve.wait_ge(s["setup_step"], 1)
                v.tensor_copy(add1[:], add1_b[:].rearrange("p (b o j) -> p b o j", b=B, o=1)
                              .to_broadcast([1, B, G, J]))
                v.tensor_scalar(wr_now[:], wr_sb, mu_r_sb, None, ALU.mult)
                v.tensor_scalar(wr_prev[:], wr_sb, one_mu[:], None, ALU.mult)
                v.tensor_scalar(wv_half[:], wv_sb, 0.5, None, ALU.mult)
                dve.wait_ge(s["k1_mm"], 1)
                v.tensor_scalar(k1[:], pr_bank[:, 0:B * J].rearrange("p (b j) -> p b j", j=J), 0.0, diag_sb,
                                ALU.max, ALU.mult).then_inc(s["setup_dve"], 1)

            st_count = [0]

            def st_step(ins):
                ins.then_inc(s["st"], 1)
                st_count[0] += 1
                dve.wait_ge(s["st"], st_count[0])

            def stats_of(n, src, signal, also_xn=False):
                for t in range(G):
                    last = v.bn_stats(stats[n][:, t, :], src[n][:, t, :])
                st_step(last)
                for t in range(G):
                    last = v.bn_aggr(mv[n][:, t, :], stats[n][:, t, :])
                st_step(last)
                if also_xn:
                    v.tensor_scalar(ve[n][:, 1], mv[n][:, :, 1], 1.0 + RMS_EPS, LN_EPS * RMS_EPS, ALU.mult, ALU.add)
                v.tensor_scalar(ve[n][:, 0], mv[n][:, :, 1], LN_EPS, None, ALU.add).then_inc(s[signal], 1)

            def shift_of(n, ready, signal, row=0):
                dve.wait_ge(s[ready], n + 1)
                v.scalar_tensor_tensor(shift[n][:], mv[n][:, :, 0], -1.0, rstd[n][:, row], ALU.mult, ALU.mult
                                       ).then_inc(s[signal], 1)

            def norm(dst, src, n, factor, signal):
                for t in range(G):
                    v.tensor_scalar(dst[n][:, t, :], src[n][:, t, :], mv[n][:, t, 0:1], factor[:, t:t + 1],
                                    ALU.subtract, ALU.mult).then_inc(s[signal], 1)

            def a_stats(n):
                dve.wait_ge(x_in[n], 16)
                stats_of(n, xg, "ve")

            def a_shift(n):
                shift_of(n, "rstd", "shift")

            def a_mask(n):
                dve.wait_ge(s["cap_done"], 1)
                dve.wait_ge(s["qs"], n + 1)
                for h in range(2):
                    last = v.tensor_tensor(sm[n][:, 2 * h:2 * h + 2, :], scores0(n, h)[:, :, D:D + J],
                                           cap[:, 2 * h:2 * h + 2, :], ALU.min)
                last.then_inc(s["sm"], 1)
                dve.wait_ge(s["sm"], n + 1)
                v.tensor_reduce(nmax[n][:], sm[n][:], axis=AX.X, op=ALU.max, negate=True).then_inc(s["max"], 1)

            def a_soft(n):
                dve.wait_ge(s["exp"], n + 1)
                v.reciprocal(rinv[n][:], rsum[n][:]).then_inc(s["rinv"], 1)
                dve.wait_ge(s["rinv"], n + 1)
                v.tensor_tensor(pr[n][:], pr[n][:],
                                rinv[n][:].rearrange("p (t o) -> p t o", o=1).to_broadcast([P, G, J]),
                                ALU.mult).then_inc(s["pr"], 1)

            def a_res(n):
                dve.wait_ge(s["pv"], n + 1)
                for h in range(2):
                    last = v.tensor_tensor(x1[n][:, 2 * h:2 * h + 2, :], scores0(n, h)[:, :, 0:D],
                                           xg[n][:, 2 * h:2 * h + 2, :], ALU.add)
                last.then_inc(s["x1"], 1)

            def a_stats2(n):
                dve.wait_ge(s["x1"], n + 1)
                stats_of(n, x1, "ve2", also_xn=True)

            def a_shift2(n):
                shift_of(n, "rstd_x", "shift2", 1)

            def a_scores(n):
                dve.wait_ge(s["rt"], n + 1)
                v.tensor_copy(sc[:, n * G:(n + 1) * G, :], route_bank[:, 0:G * E].rearrange("p (t e) -> p t e", e=E)
                              ).then_inc(s["sc_sb"], 1)

            steps = [0]

            def step(ins):
                ins.then_inc(s["step"], 1)
                steps[0] += 1
                dve.wait_ge(s["step"], steps[0])

            def a_choose(n):
                tiles = slice(n * G, (n + 1) * G)

                def wide(a):
                    return a[:, tiles].rearrange("p (t o) -> p t o", o=1).to_broadcast([P, G, E])

                dve.wait_ge(s["sc_sb"], n + 1)
                for k, src, top, pick in ((0, sc, top1, pick1), (1, sc2, top2, pick2)):
                    step(v.tensor_reduce(top[:, tiles], src[:, tiles], axis=AX.X, op=ALU.max))
                    step(v.tensor_tensor(eq[:, tiles], src[:, tiles], wide(top), ALU.is_equal))
                    step(v.tensor_tensor(eq[:, tiles], eq[:, tiles], first_w[:, tiles], ALU.mult))
                    step(v.tensor_reduce(pick[:, tiles], eq[:, tiles], axis=AX.X, op=ALU.max))
                    step(v.tensor_tensor(hot[:, k, tiles], first_w[:, tiles], wide(pick), ALU.is_equal))
                    if k == 0:
                        step(v.scalar_tensor_tensor(sc2[:, tiles], hot[:, 0, tiles], -FREE, sc[:, tiles],
                                                    ALU.mult, ALU.add))
                v.tensor_tensor(hot16[:, tiles], hot[:, 0, tiles], hot[:, 1, tiles], ALU.add
                                ).then_inc(s["hot_done"], 1)
                v.tensor_tensor(dist[:, tiles], sc[:, tiles], wide(top1), ALU.subtract)
                v.tensor_tensor(top2[:, tiles], top2[:, tiles], top1[:, tiles], ALU.subtract
                                ).then_inc(s["dist_done"], 1)

            for stage, n in staggered(((3, a_stats), (5.5, a_shift), (11, a_mask), (13.3, a_soft), (14.6, a_res),
                                       (17.1, a_stats2), (19.1, a_shift2), (23.4, a_scores),
                                       (24.2, a_choose)), LAG0):
                if stage is a_mask and n == 0:
                    setup_rest()
                stage(n)

            dve.wait_ge(s["prefix_mm"], 1)
            v.tensor_copy(counts[:], banks[1][:, 0:P]).then_inc(s["counts_done"], 1)
            dve.wait_ge(s["totals_mm"], 1)
            totals = banks[2][:, 0:E].rearrange("p (e o) -> p e o", o=1).to_broadcast([P, E, T // P])
            steps_wide = step_no.rearrange("p (o c) -> p o c", o=1).to_broadcast([P, E, T // P])
            step(v.tensor_tensor(n_gt[:], totals, steps_wide, ALU.is_gt))
            step(v.tensor_reduce(n_blocks[:], n_gt[:], axis=AX.X, op=ALU.add))
            step(v.tensor_tensor(tri[:], lower, n_blocks[:].rearrange("p (o f) -> p o f", o=1)
                                 .to_broadcast([P, E, E]), ALU.mult))
            step(v.tensor_reduce(start_pos[:], tri[:], axis=AX.X, op=ALU.add))
            step(v.tensor_tensor(pos_e[:], banks[0][:, 0:TILES * E].rearrange("p (t e) -> p t e", e=E),
                                 start_pos[:].rearrange("p (o e) -> p o e", o=1).to_broadcast([P, TILES, E]),
                                 ALU.add))
            v.tensor_tensor(pos_m[:, 0], pos_e[:], hot[:, 0], ALU.mult)
            step(v.tensor_tensor(pos_m[:, 1], pos_e[:], hot[:, 1], ALU.mult))
            step(v.tensor_reduce(pos[:], pos_m[:].rearrange("p k t e -> p (k t) e"), axis=AX.X, op=ALU.add))
            step(v.tensor_copy(pos_i[:], pos[:]))
            v.tensor_scalar(blk_i[:], pos_i[:], P.bit_length() - 1, None, ALU.logical_shift_right)
            step(v.tensor_scalar(row_i[:], pos_i[:], P - 1, None, ALU.bitwise_and))
            v.tensor_copy(blk_h[:], blk_i[:])
            v.tensor_copy(row_h[:], row_i[:]).then_inc(s["row_done"], 1)
            dve.wait_ge(s["row_done"], 1)
            v.tensor_tensor(in_block[:], block_no, over(blk_h[:], BLOCKS), ALU.is_equal
                            ).then_inc(s["block_done"], 1)
            dve.wait_ge(s["block_done"], 1)
            v.tensor_tensor(marks[:, 0], in_block[:], over(col_no, BLOCKS), ALU.mult).then_inc(s["marks0_done"], 1)
            dve.wait_ge(s["row_no_in"], 16)
            for part in range(PARTS):
                cols = slice(part * COLS // PARTS, (part + 1) * COLS // PARTS)
                v.tensor_tensor(row_sb[:, :, cols], row_sb[:, :, cols], over(row_h[:, cols], P), ALU.is_equal
                                ).then_inc(s["inrow_done"], 1)
            step(v.scalar_tensor_tensor(end_pos[:], n_blocks[:], float(P), start_pos[:], ALU.mult, ALU.add))
            step(v.tensor_tensor(past[:], end_pos[0:1, :].rearrange("p (o e) -> p o e", o=1)
                                 .to_broadcast([1, BLOCKS, E]), block_at[0:1, :].rearrange("p (b o) -> p b o", o=1)
                                 .to_broadcast([1, BLOCKS, E]), ALU.is_le))
            step(v.tensor_reduce(expert_f[:], past[:], axis=AX.X, op=ALU.add))
            v.tensor_scalar(expert[:, 0:BLOCKS], expert_f[:], float(E - 1), None, ALU.min).then_inc(s["expert_done"], 1)
            dve.wait_ge(s["inv_mm"], 1)
            marks_sum = banks[3][:, 0:2 * BLOCKS].rearrange("p (k b) -> p b k", b=BLOCKS)
            step(v.tensor_reduce(pair_f[:], marks_sum, axis=AX.X, op=ALU.add))
            step(v.tensor_copy(pair_i[:], pair_f[:]))
            v.tensor_scalar(src_row[:], pair_i[:], T - 1, None, ALU.bitwise_and).then_inc(s["src_done"], 1)
            step(v.scalar_tensor_tensor(spare[:], pair_f[:], 0.5, spare_row, ALU.is_lt, ALU.mult))
            v.tensor_tensor(dst_row[:], pair_f[:], spare[:], ALU.add).then_inc(s["dst_done"], 1)
            dve.wait_ge(s["ex_done"], 1)
            step(v.tensor_reduce(den[:], dist[:], axis=AX.X, op=ALU.add))
            step(v.reciprocal(c_rec[:], den[:]))
            step(v.tensor_scalar(weight[:, 0], c_rec[:], 0.5, None, ALU.mult))
            v.tensor_tensor(weight[:, 1], weight[:, 0], top2[:], ALU.mult).then_inc(s["weight_done"], 1)

            def silu(b, par):
                dve.wait_ge(s["b_th"], b + 1)
                v.scalar_tensor_tensor(gs[par][:], th[par][:], 1.0, gate[par][:, 0:H], ALU.add, ALU.mult
                                       ).then_inc(s["b_gs"], 1)
                dve.wait_ge(s["b_gs"], b + 1)
                v.tensor_tensor(hid[par][:, 0:H], gs[par][:], val[par][:, 0:H], ALU.mult
                                ).then_inc(s["b_hid"], 1)

            def low_rows(b, par):
                dve.wait_ge(s["b_xt"], b + 1)
                v.scalar_tensor_tensor(rows_lo[par][:], rt_bank[par][:, 0:P], scale_sb, rows_hi[par][:].bitcast(F32),
                                       ALU.mult, ALU.subtract).then_inc(s["b_lo"], 1)

            def move_y(b, m, par):
                dve.wait_ge(s["b_dn"], b + 1)
                dve.wait_ge(s["ys_free"], b + 1)
                v.tensor_copy(ys[m][:], ht_bank[par][:, HP:HP + D]).then_inc(s["b_y"], 1)

            dve.wait_ge(s["zeroed"], 1)
            low_rows(0, 0)
            low_rows(1, 1)
            silu(0, 0)
            low_rows(2, 0)
            silu(1, 1)
            low_rows(3, 1)
            with dve.Fori(2, LOOP_END, UNROLL) as i:
                for j in range(UNROLL):
                    b, par = i + j, j % 2
                    move_y(b - 2, j % RING, par)
                    silu(b, par)
                    low_rows(b + 2, par)
            for b in range(LOOP_END, BLOCKS):
                move_y(b - 2, (b - 2) % RING, b % 2)
                silu(b, b % 2)
                if b + 2 < BLOCKS:
                    low_rows(b + 2, b % 2)
            for c in (b - 1, b):
                move_y(c, c % RING, c % 2)

            def c_combine(n):
                dve.wait_ge(s["skip"], n + 1)
                if n == 0:
                    dve.wait_ge(s["weight_done"], 1)
                for k, onto in ((0, skip), (1, xg)):
                    dve.wait_ge(yb_in[n][k], 16)
                    if k:
                        dve.wait_ge(s["c_step"], n + 1)
                    for t in range(G):
                        last = v.scalar_tensor_tensor(xg[n][:, t, :], yb[n % 2][:, k, t, :],
                                                      weight[:, k, n * G + t:n * G + t + 1], onto[n][:, t, :],
                                                      ALU.mult, ALU.add)
                    last.then_inc(s["c_x2" if k else "c_step"], 1)

            def c_stats(n):
                dve.wait_ge(s["c_x2"], n + 1)
                stats_of(n, xg, "c_ve")

            def c_shift(n):
                shift_of(n, "c_rstd", "c_shift")

            def c_max(n):
                dve.wait_ge(s["c_sc"], n + 1)
                v.tensor_reduce(nmax[n][:], c_at_bank[:, 0:G * J].rearrange("p (t j) -> p t j", j=J), axis=AX.X,
                                op=ALU.max, negate=True).then_inc(s["c_max"], 1)

            def c_recip(n):
                dve.wait_ge(s["c_exp"], n + 1)
                v.reciprocal(rinv[n][:], rsum[n][:]).then_inc(s["c_rinv"], 1)

            def c_res(n):
                dve.wait_ge(s["c_rinv"], n + 1)
                dve.wait_ge(s["c_pv"], n + 1)
                for t in range(G):
                    last = v.scalar_tensor_tensor(x1[n][:, t, :], c_pv_bank[:, t * D:(t + 1) * D],
                                                  rinv[n][:, t:t + 1], xg[n][:, t, :], ALU.mult, ALU.add)
                last.then_inc(s["c_x3"], 1)

            def c_stats4(n):
                dve.wait_ge(s["c_x3"], n + 1)
                stats_of(n, x1, "c_ve4")

            def c_z(n):
                dve.wait_ge(s["c_rstd4"], n + 1)
                norm(xh, x1, n, rstd[n][:, 0], "c_z")

            def c_mix(n):
                dve.wait_ge(s["c_dz"], n + 1)
                if n >= 2:
                    dve.wait_ge(s["c_k"], n - 1)
                v.scalar_tensor_tensor(xk[n % 2][:], dz[n % 2][:], mu_k_sb, xt[n][:, 0:S], ALU.mult, ALU.add
                                       ).then_inc(s["c_xk"], 1)

            def c_gate(n):
                dve.wait_ge(s["c_tg"], n + 1)
                dve.wait_ge(s["c_kv"], n + 1)
                xh_n = xh[n][:].rearrange("p t d -> p (t d)")
                v.scalar_tensor_tensor(xh_n, xh_n, 1.0, c_kv_bank[:], ALU.add, ALU.mult).then_inc(s["c_wv"], 1)
                if n == B - 1:
                    dve.wait_ge(s["c_wv"], n + 1)
                    v.tensor_tensor(xh[n][:], xh[n][:], x1[n][:], ALU.add).then_inc(s["c_last"], 1)

            for stage, n in staggered(((3.3, c_combine), (4.8, c_stats), (6.5, c_shift), (11.6, c_max),
                                       (15.6, c_recip), (16.7, c_res), (17.3, c_stats4), (19.6, c_z), (21.6, c_mix),
                                       (26.4, c_gate)), LAG1):
                stage(n)


def shape_constants():
    c = np.zeros((P, C_ALL), np.float32)
    p = np.arange(P)
    c[:, C_IDENT:C_FIRST] = np.eye(P)
    c[:, C_FIRST:C_LOWER] = np.tile(E - np.arange(E), TILES)
    c[:, C_LOWER:C_BLOCK] = P * np.tril(np.ones((E, E)), -1).reshape(-1)
    c[:, C_BLOCK:C_SPARE] = np.arange(BLOCKS) * P
    c[:, C_SPARE:C_STEP] = P + PAIRS + np.arange(BLOCKS) * P + p[:, None]
    c[:, C_STEP:C_LANE] = np.arange(T // P) * P
    c[:, C_LANE] = p
    m = np.zeros((P, M_ALL), np.float16)
    tile_of, expert_of = np.divmod(np.arange(TILES * E), E)
    m[:, M_BEFORE:M_ONES] = p[:, None] < p
    m[:, M_ONES:M_EARLIER] = 1
    m[:, M_EARLIER:M_SAME] = (expert_of[:, None] == expert_of) & (tile_of[:, None] < tile_of)
    m[:, M_SAME:M_BLOCK] = expert_of[:, None] == np.arange(E)
    m[:, M_BLOCK:M_COL] = np.repeat(np.arange(BLOCKS), COLS)
    m[:, M_COL:M_ALL] = P * (1 + np.arange(COLS))
    rows = np.broadcast_to(np.repeat(p, COLS), (P, P * COLS)).astype(np.float16)
    return c, m, rows


def kernel(**inputs):
    import concourse.bacc as bacc
    from concourse.bass_utils import run_bass_kernel_spmd

    a = {k: np.asarray(v) for k, v in inputs.items()}
    consts, small, row_no = shape_constants()
    mask = a["mask_1xSxS2_bk0"].reshape(G, P, J).transpose(1, 0, 2)
    arrays = {
        "x": a["x"].reshape(T, D),
        "ctx": a["ctx_1024"].transpose(1, 0, 2),
        "attn_mask": mask,
        "row_mask": a["mask_BxS2_if1"].reshape(1, B * J),
        "keys": np.concatenate((a["L0_xattn_wi"], a["L0_xattn_wi"].T, a["ctx_1024"].reshape(B * J, D).T), axis=1),
        "weights": np.concatenate((
            a["L1_xattn_W"].T, a["L1_ffn_W_r"].T, a["L1_ffn_W_k"].T, a["L1_ffn_W_v"].T, a["L0_ffn_w_router"].T,
            a["L0_ffn_norm_scale"].reshape(D, 1), a["L1_xattn_diagonal"].reshape(D, 1),
            a["L1_ffn_mu_r"].reshape(D, 1), a["L1_ffn_mu_k"].reshape(D, 1)), axis=1),
        "up_t": a["L0_ffn_w_up"].transpose(2, 0, 1),
        "down_t": a["L0_ffn_w_down"].transpose(2, 0, 1),
        "consts": consts,
        "small": small,
        "row_no": row_no,
    }
    arrays = {k: np.ascontiguousarray(v) for k, v in arrays.items()}
    nc = bacc.Bacc("TRN2", target_bir_lowering=False, num_devices=1)
    aps = [nc.dram_tensor(f"in_{k}", v.shape, mybir.dt.from_np(v.dtype), kind="ExternalInput").ap()
           for k, v in arrays.items()]
    out = nc.dram_tensor("out_rows", (T, D), F32, kind="ExternalOutput").ap()
    build(nc, *aps, out)
    r = run_bass_kernel_spmd(nc, [{f"in_{k}": v for k, v in arrays.items()}], core_ids=[0])
    return r.results[0]["out_rows"].reshape(B, S, D)
```
